# Optimizing a Trainium2 kernel written in Bass

```python
import numpy as np
import jax
import jax.numpy as jnp

def _softmax(x, axis=-1):
    return jax.nn.softmax(x, axis=axis)

def _gelu(x):
    return jax.nn.gelu(x, approximate=True)

def _silu(x):
    return jax.nn.silu(x)

def _sigmoid(x):
    return jax.nn.sigmoid(x)

def _layernorm(x, axis=-1, eps=1e-05):
    m = jnp.mean(x, axis=axis, keepdims=True)
    v = jnp.var(x, axis=axis, keepdims=True)
    return (x - m) / jnp.sqrt(v + eps)

def _scatter_add(tgt, idx, src, axis=0):
    return tgt.at[idx].add(src)

def _segment_sum(src, seg, n):
    return jax.ops.segment_sum(src, seg, n)
kernel_name = 'mk_recurrent_d1_jaxref_r8_b679c6'

def setup_inputs(seed: int=0):
    np.random.seed(seed)
    _w = jnp.asarray

    def _L0_attn_setup():
        import jax, jax.numpy as jnp
        import numpy as np
        B, T, D, H, K, V, F = (4, 512, 128, 8, 128, 128, 512)
        EPS = 1e-05

        def layernorm(x, w, b):
            m = jnp.mean(x, -1, keepdims=True)
            v = jnp.var(x, -1, keepdims=True)
            return (x - m) * jax.lax.rsqrt(v + EPS) * w + b

        def l2norm(x):
            return x * jax.lax.rsqrt(jnp.sum(x * x, -1, keepdims=True) + 1e-06)

        def gdn_recurrence(q, k, v, alpha, beta):
            qT = jnp.moveaxis(q, 1, 0)
            kT = jnp.moveaxis(k, 1, 0)
            vT = jnp.moveaxis(v, 1, 0)
            aT = jnp.moveaxis(alpha, 1, 0)
            bT = jnp.moveaxis(beta, 1, 0)

            def step(S, inp):
                q_t, k_t, v_t, a_t, b_t = inp
                kS = jnp.einsum('bhk,bhkv->bhv', k_t, S)
                bk = (b_t[..., None] * k_t)[..., :, None]
                S = a_t[..., None, None] * (S - bk * kS[..., None, :]) + bk * v_t[..., None, :]
                o = jnp.einsum('bhk,bhkv->bhv', q_t, S)
                return (S, o)
            S0 = jnp.zeros((q.shape[0], H, K, V), q.dtype)
            _, oT = jax.lax.scan(step, S0, (qT, kT, vT, aT, bT))
            return jnp.moveaxis(oT, 0, 1)
        key = jax.random.key(seed)
        ks = jax.random.split(key, 12)
        s = 0.02
        return {'x': jax.random.normal(ks[0], (B, T, D), jnp.float32), 'Wq': jax.random.normal(ks[1], (D, H * K), jnp.float32) * s, 'Wk': jax.random.normal(ks[2], (D, H * K), jnp.float32) * s, 'Wv': jax.random.normal(ks[3], (D, H * V), jnp.float32) * s, 'Wb': jax.random.normal(ks[4], (D, H), jnp.float32) * s, 'Wa': jax.random.normal(ks[5], (D, H), jnp.float32) * s, 'Wo': jax.random.normal(ks[6], (H * V, D), jnp.float32) * s, 'ln1_w': jnp.ones((D,), jnp.float32), 'ln1_b': jnp.zeros((D,), jnp.float32), 'ln2_w': jnp.ones((D,), jnp.float32), 'ln2_b': jnp.zeros((D,), jnp.float32), 'W1': jax.random.normal(ks[7], (D, F), jnp.float32) * s, 'b1': jnp.zeros((F,), jnp.float32), 'W2': jax.random.normal(ks[8], (F, D), jnp.float32) * s, 'b2': jnp.zeros((D,), jnp.float32)}
    _L0_attn_in = _L0_attn_setup()

    def _L0_ffn_setup():
        import jax, jax.numpy as jnp
        import numpy as np
        H = 128
        I = 64
        E = 32
        TOP_K = 6
        N_GROUP = 8
        TOPK_GROUP = 4
        SCALE = 2.5
        N_SHARED = 2
        SI = I * N_SHARED
        B, S = (2, 128)
        key = jax.random.key(seed)
        ks = jax.random.split(key, 8)
        x = jax.random.normal(ks[0], (B, S, H), jnp.float32)
        gate_weight = jax.random.normal(ks[1], (E, H), jnp.float32) * 0.02
        e_score_correction_bias = jax.random.normal(ks[2], (E,), jnp.float32) * 0.01
        experts_gate_up = jax.random.normal(ks[3], (E, 2 * I, H), jnp.float32) * 0.02
        experts_down = jax.random.normal(ks[4], (E, H, I), jnp.float32) * 0.02
        shared_gate_w = jax.random.normal(ks[5], (SI, H), jnp.float32) * 0.02
        shared_up_w = jax.random.normal(ks[6], (SI, H), jnp.float32) * 0.02
        shared_down_w = jax.random.normal(ks[7], (H, SI), jnp.float32) * 0.02
        return {'x': x, 'gate_weight': gate_weight, 'e_score_correction_bias': e_score_correction_bias, 'experts_gate_up': experts_gate_up, 'experts_down': experts_down, 'shared_gate_w': shared_gate_w, 'shared_up_w': shared_up_w, 'shared_down_w': shared_down_w}
    _L0_ffn_in = _L0_ffn_setup()
    _d = {'L0_attn_x': _L0_attn_in['x'], 'L0_attn_Wq': _L0_attn_in['Wq'], 'L0_attn_Wk': _L0_attn_in['Wk'], 'L0_attn_Wv': _L0_attn_in['Wv'], 'L0_attn_Wb': _L0_attn_in['Wb'], 'L0_attn_Wa': _L0_attn_in['Wa'], 'L0_attn_Wo': _L0_attn_in['Wo'], 'L0_attn_ln1_w': _L0_attn_in['ln1_w'], 'L0_attn_ln1_b': _L0_attn_in['ln1_b'], 'L0_attn_ln2_w': _L0_attn_in['ln2_w'], 'L0_attn_ln2_b': _L0_attn_in['ln2_b'], 'L0_attn_W1': _L0_attn_in['W1'], 'L0_attn_b1': _L0_attn_in['b1'], 'L0_attn_W2': _L0_attn_in['W2'], 'L0_attn_b2': _L0_attn_in['b2'], 'L0_ffn_gate_weight': _L0_ffn_in['gate_weight'], 'L0_ffn_e_score_correction_bias': _L0_ffn_in['e_score_correction_bias'], 'L0_ffn_experts_gate_up': _L0_ffn_in['experts_gate_up'], 'L0_ffn_experts_down': _L0_ffn_in['experts_down'], 'L0_ffn_shared_gate_w': _L0_ffn_in['shared_gate_w'], 'L0_ffn_shared_up_w': _L0_ffn_in['shared_up_w'], 'L0_ffn_shared_down_w': _L0_ffn_in['shared_down_w']}
    _x0 = _d['L0_attn_x']
    _d['L0_attn_x'] = jax.random.normal(jax.random.fold_in(jax.random.key(seed), 1), (2, 2048, 128), dtype=_x0.dtype)
    del _x0
    return _d

def reference(L0_attn_x, L0_attn_Wq, L0_attn_Wk, L0_attn_Wv, L0_attn_Wb, L0_attn_Wa, L0_attn_Wo, L0_attn_ln1_w, L0_attn_ln1_b, L0_attn_ln2_w, L0_attn_ln2_b, L0_attn_W1, L0_attn_b1, L0_attn_W2, L0_attn_b2, L0_ffn_gate_weight, L0_ffn_e_score_correction_bias, L0_ffn_experts_gate_up, L0_ffn_experts_down, L0_ffn_shared_gate_w, L0_ffn_shared_up_w, L0_ffn_shared_down_w):

    def _L0_attn_ref(x, Wq, Wk, Wv, Wb, Wa, Wo, ln1_w, ln1_b, ln2_w, ln2_b, W1, b1, W2, b2):
        import jax, jax.numpy as jnp
        import numpy as np
        B, T, D, H, K, V, F = (4, 512, 128, 8, 128, 128, 512)
        EPS = 1e-05

        def layernorm(x, w, b):
            m = jnp.mean(x, -1, keepdims=True)
            v = jnp.var(x, -1, keepdims=True)
            return (x - m) * jax.lax.rsqrt(v + EPS) * w + b

        def l2norm(x):
            return x * jax.lax.rsqrt(jnp.sum(x * x, -1, keepdims=True) + 1e-06)

        def gdn_recurrence(q, k, v, alpha, beta):
            qT = jnp.moveaxis(q, 1, 0)
            kT = jnp.moveaxis(k, 1, 0)
            vT = jnp.moveaxis(v, 1, 0)
            aT = jnp.moveaxis(alpha, 1, 0)
            bT = jnp.moveaxis(beta, 1, 0)

            def step(S, inp):
                q_t, k_t, v_t, a_t, b_t = inp
                kS = jnp.einsum('bhk,bhkv->bhv', k_t, S)
                bk = (b_t[..., None] * k_t)[..., :, None]
                S = a_t[..., None, None] * (S - bk * kS[..., None, :]) + bk * v_t[..., None, :]
                o = jnp.einsum('bhk,bhkv->bhv', q_t, S)
                return (S, o)
            S0 = jnp.zeros((q.shape[0], H, K, V), q.dtype)
            _, oT = jax.lax.scan(step, S0, (qT, kT, vT, aT, bT))
            return jnp.moveaxis(oT, 0, 1)
        b, t, _ = x.shape
        n = layernorm(x, ln1_w, ln1_b)
        q = l2norm(jax.nn.silu(n @ Wq).reshape(b, t, H, K))
        k = l2norm(jax.nn.silu(n @ Wk).reshape(b, t, H, K))
        v = jax.nn.silu(n @ Wv).reshape(b, t, H, V)
        beta = jax.nn.sigmoid(n @ Wb)
        alpha = jax.nn.sigmoid(n @ Wa)
        o = gdn_recurrence(q, k, v, alpha, beta).reshape(b, t, H * V) @ Wo
        x = x + o
        h = layernorm(x, ln2_w, ln2_b)
        x = x + (jax.nn.gelu(h @ W1 + b1, approximate=False) @ W2 + b2)
        return x

    def _L0_ffn_ref(x, gate_weight, e_score_correction_bias, experts_gate_up, experts_down, shared_gate_w, shared_up_w, shared_down_w):
        import jax, jax.numpy as jnp
        import numpy as np
        H = 128
        I = 64
        E = 32
        TOP_K = 6
        N_GROUP = 8
        TOPK_GROUP = 4
        SCALE = 2.5
        N_SHARED = 2
        SI = I * N_SHARED
        B, S = (2, 128)
        b, s, h = x.shape
        xf = x.reshape(-1, h)
        T = xf.shape[0]
        logits = xf.astype(jnp.float32) @ gate_weight.astype(jnp.float32).T
        scores = jax.nn.sigmoid(logits)
        sfc = scores + e_score_correction_bias[None, :]
        gs = E // N_GROUP
        group_scores = sfc.reshape(T, N_GROUP, gs).max(axis=-1)
        _, gidx = jax.lax.top_k(group_scores, TOPK_GROUP)
        gmask = jnp.zeros((T, N_GROUP), bool).at[jnp.arange(T)[:, None], gidx].set(True)
        smask = jnp.repeat(gmask, gs, axis=1)
        masked = jnp.where(smask, sfc, 0.0)
        _, topk_idx = jax.lax.top_k(masked, TOP_K)
        tw = jnp.take_along_axis(scores, topk_idx, axis=1)
        tw = tw / (tw.sum(-1, keepdims=True) + 1e-20)
        tw = (tw * SCALE).astype(xf.dtype)
        combine = jnp.zeros((T, E), xf.dtype).at[jnp.arange(T)[:, None], topk_idx].add(tw)

        def expert_step(acc, inp):
            gu, dn, c = inp
            g = xf @ gu[:I].T
            u = xf @ gu[I:].T
            o = jax.nn.silu(g) * u @ dn.T
            return (acc + c[:, None] * o, None)
        routed, _ = jax.lax.scan(expert_step, jnp.zeros_like(xf), (experts_gate_up, experts_down, combine.T))
        sh = jax.nn.silu(xf @ shared_gate_w.T) * (xf @ shared_up_w.T)
        shared_out = sh @ shared_down_w.T
        return (routed + shared_out).reshape(b, s, h)
    x = L0_attn_x
    xn = _layernorm(x, axis=-1)
    s = _L0_attn_ref(xn, L0_attn_Wq, L0_attn_Wk, L0_attn_Wv, L0_attn_Wb, L0_attn_Wa, L0_attn_Wo, L0_attn_ln1_w, L0_attn_ln1_b, L0_attn_ln2_w, L0_attn_ln2_b, L0_attn_W1, L0_attn_b1, L0_attn_W2, L0_attn_b2)
    g = _silu(_L0_ffn_ref(xn, L0_ffn_gate_weight, L0_ffn_e_score_correction_bias, L0_ffn_experts_gate_up, L0_ffn_experts_down, L0_ffn_shared_gate_w, L0_ffn_shared_up_w, L0_ffn_shared_down_w))
    x = x + s * g
    return x

_drawn_inputs = setup_inputs


def setup_inputs(seed=0):
    import zlib

    import numpy as np

    out = dict(_drawn_inputs(seed))
    spreads = {'L0_attn_ln1_w': (1.0, 0.6),
     'L0_attn_ln1_b': (0.0, 0.8),
     'L0_attn_ln2_w': (1.0, 0.6),
     'L0_attn_ln2_b': (0.0, 0.8),
     'L0_attn_b1': (0.0, 0.8),
     'L0_attn_b2': (0.0, 0.8)}
    factors = {'L0_attn_Wq': 8.0,
     'L0_attn_Wk': 8.0,
     'L0_attn_Wv': 8.0,
     'L0_attn_Wb': 8.0,
     'L0_attn_Wa': 8.0,
     'L0_attn_Wo': 8.0,
     'L0_attn_W1': 8.0,
     'L0_attn_W2': 8.0,
     'L0_ffn_gate_weight': 8.0,
     'L0_ffn_e_score_correction_bias': 8.0,
     'L0_ffn_experts_gate_up': 8.0,
     'L0_ffn_experts_down': 8.0,
     'L0_ffn_shared_gate_w': 8.0,
     'L0_ffn_shared_up_w': 8.0,
     'L0_ffn_shared_down_w': 8.0}
    for name, (base, spread) in spreads.items():
        noise = np.random.default_rng([zlib.crc32(name.encode()), seed]).standard_normal(out[name].shape)
        drawn = base * np.exp(spread * noise) if base else spread * noise
        out[name] = jnp.asarray(drawn.astype(out[name].dtype))
    for name, factor in factors.items():
        out[name] = (out[name] * factor).astype(out[name].dtype)
    return out
```

```python
from contextlib import ExitStack

import numpy as np

import concourse.bass as bass
from concourse import mybir

ALU = mybir.AluOpType
ACT = mybir.ActivationFunctionType
F32 = mybir.dt.float32
BF16 = mybir.dt.bfloat16
AX_X = mybir.AxisListType.X

P = 128
HALF = 4
W4 = HALF * P
EPS = 1e-5
L2EPS = 1e-6
LEVELS = (2, 4, 8, 16, 32, 64)
RING = 8
BIG = 30000.0


class Stage:

    def __init__(self, reg, factor, const):
        self.reg, self.factor, self.const = reg, factor, const

    def __sub__(self, n):
        return Stage(self.reg, self.factor, self.const - n)

    def __add__(self, n):
        return self - (-n)

    def done(self, part=1, of=1):
        c = of * self.const + part
        return c if self.reg is None else self.reg * (of * self.factor) + c

    def group(self, half):
        return Stage(self.reg, 2 * self.factor, 2 * self.const + half)

    def turn(self, n):
        return Stage(self.reg, self.factor // n, self.const // n)

    def tile(self):
        return self.turn(2)


def build(nc, x, wqkv, wba, wo, ln1, ln2, w1, b1, w2, b2, gate_t, ecb, gu, down, sh_gu, sh_down,
          c_ident, c_incl, c_after, c_level, c_init, c_below, out):
    B, T, D = x.shape
    H = wo.shape[1]
    F = w1.shape[1]
    FB = F // P
    E = gate_t.shape[1]
    I = down.shape[1]
    NG, KG, TOPK, SCALE = 8, 4, 6, 2.5
    EG = E // NG
    GB = E * I // W4
    KT = E * I // P
    HALVES = H // HALF
    STEPS = T // P
    TILES = B * STEPS
    GROUPS = TILES * HALVES
    assert D == P and B == 2 and HALVES == 2 and GROUPS % RING == 0
    LAGC = 2
    LAGF = 4
    NL = len(LEVELS)

    with ExitStack() as ctx:
        def sb(name, shape, dt=F32):
            return ctx.enter_context(nc.sbuf_tensor(name, shape, dt))

        def ps(name):
            return ctx.enter_context(nc.psum_tensor(name, [P, W4], F32))

        wqkv_sb = sb("wqkv_sb", [P, 3, H * P])
        wba_sb = sb("wba_sb", [P, 2 * H])
        wo_sb = sb("wo_sb", [P, H, P])
        ln1_sb = sb("ln1_sb", [P, 2])
        ln2_sb = sb("ln2_sb", [P, 2])
        w1_sb = sb("w1_sb", [P, F])
        b1_sb = sb("b1_sb", [P, FB])
        w2_sb = sb("w2_sb", [P, FB, P])
        b2_sb = sb("b2_sb", [P, P])
        gate_sb = sb("gate_sb", [P, E])
        ecb_sb = sb("ecb_sb", [P, E])
        gu_sb = sb("gu_sb", [P, 2, E * I])
        down_sb = sb("down_sb", [P, KT, P])
        shgu_sb = sb("shgu_sb", [P, 2, P])
        shdown_sb = sb("shdown_sb", [P, P])
        ident = sb("ident", [P, P])
        incl = sb("incl", [P, P])
        after = sb("after", [P, P])
        level = sb("level", [P, NL, P])
        winit = sb("winit", [P, P])
        ones = sb("ones", [P, P])
        nhalf = sb("nhalf", [P, 2 * HALF])
        identb = sb("identb", [P, P], BF16)
        below = sb("below", [P, P], BF16)

        xin = sb("xin", [P, 4, P])
        xn = sb("xn", [P, 4, P])
        n0 = sb("n0", [P, P])
        stat = sb("stat", [P, 4, 6])
        mv = sb("mv", [P, 4, 2])
        rstd = sb("rstd", [P, 4, 2])
        xnT = sb("xnT", [P, 2, P])
        nT = sb("nT", [P, 2, P])
        NZ = 2 * H + E
        zm = sb("zm", [P, NZ])
        nz = sb("nz", [P, H])
        ez = sb("ez", [P, NZ])
        ez1 = sb("ez1", [P, NZ])
        sg = sb("sg", [P, 2, H + E])
        lnz = sb("lnz", [P, H])
        la = sb("la", [P, 2, H])
        dec = sb("dec", [P, 4, 3 * H])
        sfc = sb("sfc", [P, E])
        gmx = sb("gmx", [P, NG])
        top = sb("top", [P, 8])
        gt = sb("gt", [P, E])
        cnt = sb("cnt", [P, 2])
        eqa = sb("eqa", [P, 16 + E])
        eqb = sb("eqb", [P, 16 + E])
        eqc = sb("eqc", [P, 16 + E])
        eq = sb("eq", [P, E])
        chosen = sb("chosen", [P, E])
        gmask = sb("gmask", [P, NG])
        masked = sb("masked", [P, E])
        wsel = sb("wsel", [P, E])
        wsum = sb("wsum", [P, 2])
        comb = sb("comb", [P, 2, E])
        qk = sb("qk", [P, 2, 2, W4])
        qk2 = sb("qk2", [P, 2, W4])
        ssq = sb("ssq", [P, 2 * HALF])
        rn = sb("rn", [P, 3, 2 * HALF])
        hat = sb("hat", [P, 3, W4])
        v = sb("v", [P, 4, W4])
        kdec = sb("kdec", [P, 4, W4])
        kqT = sb("kqT", [P, 4, HALF, 2, P])
        qgT = sb("qgT", [P, 4, W4])
        rhsD = sb("rhsD", [P, W4])
        expD = sb("expD", [P, W4])
        decay = sb("decay", [P, W4])
        MA = sb("MA", [P, 4, HALF, 2, P])
        Wt = sb("Wt", [P, 4, W4])
        Tm = sb("Tm", [P, W4])
        Qm = sb("Qm", [P, W4])
        S = sb("S", [P, B, H, P])
        R = sb("R", [P, W4])
        U = sb("U", [P, W4])
        OT = sb("OT", [P, 4, W4])
        sgm = sb("sgm", [P, 2, W4])
        hm = sb("hm", [P, 2, W4])
        hc = sb("hc", [P, 2, W4])
        hT = sb("hT", [P, KT + 1, P])
        shs = sb("shs", [P, P])
        shh = sb("shh", [P, P])
        gsil = sb("gsil", [P, 4, P])
        x1 = sb("x1", [P, P])
        x1b = sb("x1b", [P, P])
        h0 = sb("h0", [P, P])
        hT2 = sb("hT2", [P, P])
        gel = sb("gel", [P, FB, P])
        fs = sb("fs", [P, P])
        fy = sb("fy", [P, P])
        fo = sb("fo", [P, 2, P])

        psA = [ps("psA0"), ps("psA1")]
        psB = [ps("psB0"), ps("psB1")]
        psC = [ps("psC0"), ps("psC1")]
        psM = ps("psM")
        psL = ps("psL")

        def sem(name):
            return ctx.enter_context(nc.semaphore(name))

        weights = sem("weights")
        constants_ready = sem("constants_ready")
        passed = sem("passed")
        stats_ready = sem("stats_ready")
        rstd_ready = sem("rstd_ready")
        normed = sem("normed")
        norm_turned = sem("norm_turned")
        normT_ready = sem("normT_ready")
        z_done = sem("z_done")
        z_ready = sem("z_ready")
        expz_ready = sem("expz_ready")
        sigmoid_ready = sem("sigmoid_ready")
        logz_ready = sem("logz_ready")
        logalpha_ready = sem("logalpha_ready")
        cum_done = sem("cum_done")
        decays_ready = sem("decays_ready")
        routed = sem("routed")
        q_done = sem("q_done")
        k_done = sem("k_done")
        v_done = sem("v_done")
        q_ready = sem("q_ready")
        k_ready = sem("k_ready")
        v_ready = sem("v_ready")
        squares_ready = sem("squares_ready")
        sums_ready = sem("sums_ready")
        norms_ready = sem("norms_ready")
        hats_ready = sem("hats_ready")
        kdec_ready = sem("kdec_ready")
        qg_ready = sem("qg_ready")
        k_turned = sem("k_turned")
        q_turned = sem("q_turned")
        qg_turned = sem("qg_turned")
        kT_ready = sem("kT_ready")
        qT_ready = sem("qT_ready")
        qgT_ready = sem("qgT_ready")
        rhsD_ready = sem("rhsD_ready")
        D_done = sem("D_done")
        expD_ready = sem("expD_ready")
        decay_ready = sem("decay_ready")
        products_done = sem("products_done")
        MA_ready = sem("MA_ready")
        diagonal_set = sem("diagonal_set")
        W_begun = sem("W_begun")
        T_begun = sem("T_begun")
        P_done = sem("P_done")
        Q_ready = sem("Q_ready")
        T_done = sem("T_done")
        W_done = sem("W_done")
        T_ready = sem("T_ready")
        W_ready = sem("W_ready")
        KS_done = sem("KS_done")
        R_ready = sem("R_ready")
        U_done = sem("U_done")
        U_ready = sem("U_ready")
        OT_done = sem("OT_done")
        dS_done = sem("dS_done")
        OT_ready = sem("OT_ready")
        S_ready = sem("S_ready")
        egate_done = sem("egate_done")
        egate_ready = sem("egate_ready")
        eup_done = sem("eup_done")
        eh_ready = sem("eh_ready")
        ehc_ready = sem("ehc_ready")
        eh_turned = sem("eh_turned")
        ehT_ready = sem("ehT_ready")
        shared_done = sem("shared_done")
        shgate_ready = sem("shgate_ready")
        shh_ready = sem("shh_ready")
        shh_turned = sem("shh_turned")
        shhT_ready = sem("shhT_ready")
        down_done = sem("down_done")
        branch_ready = sem("branch_ready")
        x1_done = sem("x1_done")
        x1_ready = sem("x1_ready")
        x1stats_ready = sem("x1stats_ready")
        x1rstd_ready = sem("x1rstd_ready")
        h0_ready = sem("h0_ready")
        x1b_ready = sem("x1b_ready")
        h0_turned = sem("h0_turned")
        hT_ready = sem("hT_ready")
        w1_done = sem("w1_done")
        gelu_ready = sem("gelu_ready")
        w2_done = sem("w2_done")
        s_ready = sem("s_ready")
        y_ready = sem("y_ready")
        out_ready = sem("out_ready")
        x_in = [sem(f"x_in{k}") for k in range(4)]
        y_out = [sem(f"y_out{k}") for k in range(2)]

        def heads(t, n=HALF):
            return t.rearrange("p (h d) -> p h d", h=n)

        def along(t, n):
            return t.unsqueeze(2).to_broadcast([P, t.shape[1], n])

        def across(t, n):
            return t.unsqueeze(1).to_broadcast([P, n, t.shape[1]])

        loads = [(wqkv_sb, wqkv), (wba_sb, wba), (wo_sb, wo), (ln1_sb, ln1), (ln2_sb, ln2), (w1_sb, w1), (b1_sb, b1),
                 (w2_sb, w2), (gate_sb, gate_t), (gu_sb, gu), (shgu_sb, sh_gu),
                 (shdown_sb, sh_down), (ident, c_ident), (incl, c_incl), (after, c_after), (level, c_level),
                 (winit, c_init)]

        def n_(t):
            return t.const % 4

        block = ctx.enter_context(nc.Block())

        def slots(eng, begin, slot):
            begin()
            for c in range(RING):
                slot(Stage(None, RING, c))
            with eng.Fori(1, GROUPS // RING - 1) as i:
                for c in range(RING):
                    slot(Stage(i, RING, c))
            for c in range(GROUPS - RING, GROUPS + LAGF):
                slot(Stage(None, RING, c))

        def alive(st, total=GROUPS):
            return st.reg is not None or 0 <= st.const < total

        @block.sync
        def _(sp):
            for dst, src in loads:
                sp.dma_start(dst[:], src).then_inc(weights, 16)
            sp.dma_start(down_sb[:], down.rearrange("(k q) i h -> (q i) k h", q=2)).then_inc(weights, 16)
            sp.dma_start(b2_sb[:], b2.partition_broadcast(P)).then_inc(weights, 16)
            sp.dma_start(ecb_sb[:], ecb.partition_broadcast(P)).then_inc(weights, 16)

            def load(t, step):
                if alive(t - 4):
                    sp.wait_ge(out_ready, (t - 4).done())
                sp.dma_start(xin[:, n_(t), :], x[t.const % B, step, :]).then_inc(x_in[n_(t)], 16)

            def store(t, step):
                sp.wait_ge(out_ready, t.done())
                sp.dma_start(out[t.const % B, step, :], fo[:, t.const % 2, :]).then_inc(y_out[t.const % 2], 16)

            for c in range(4):
                load(Stage(None, RING // 2, c), slice(c // 2 * P, c // 2 * P + P))
            with sp.Fori(0, TILES // 4 - 1) as i:
                for c in range(4):
                    store_first = Stage(i, RING // 2, c)
                    step = i * (2 * P) + (c // 2) * P
                    store(store_first, bass.ds(step, P))
                    load(store_first + 4, bass.ds(step + 2 * P, P))
            for c in range(4):
                t = TILES - 4 + c
                step = (STEPS - 2 + c // 2) * P
                store(Stage(None, RING // 2, t), slice(step, step + P))
            for k in range(2):
                sp.wait_ge(y_out[k], 16 * TILES // 2)
        n_weights = 16 * (len(loads) + 3)

        @block.tensor
        def _(pe):
            def begin():
                pe.wait_ge(weights, n_weights)
                pe.wait_ge(constants_ready, 1)
                start_T(Stage(None, RING // 2, 0))
                start_z(Stage(None, RING // 2, 0))
                start_cum(Stage(None, RING // 2, 0))

            def start_T(t):
                pe.wait_ge(normed, t.done(2, 2))
                if alive(t - 1):
                    pe.wait_ge(decays_ready, (t - 1).done())
                nc.tensor.transpose(psL[:, 0:P], xn[:, n_(t), :], ident[:])
                nc.tensor.transpose(psL[:, P:2 * P], n0[:], ident[:]).then_inc(norm_turned, 1)

            def start_z(t):
                pe.wait_ge(normT_ready, t.done(2, 2))
                k = t.const % 2
                nc.tensor.matmul(psL[:, 0:H], nT[:, k, :], wba_sb[:, 0:H], start=True, stop=True)
                nc.tensor.matmul(psL[:, H + E:NZ], nT[:, k, :], wba_sb[:, H:2 * H], start=True, stop=True)
                nc.tensor.matmul(psL[:, H:H + E], xnT[:, k, :], gate_sb[:], start=True, stop=True).then_inc(z_done, 1)

            def start_cum(t):
                pe.wait_ge(logalpha_ready, t.done())
                k = t.const % 2
                for j, m in enumerate((incl, after, ones)):
                    o = NZ + 16 + j * H
                    last = nc.tensor.matmul(psL[:, o:o + H], m[:], la[:, k, :], start=True, stop=True)
                last.then_inc(cum_done, 1)

            def project(s, what, bank):
                t = s.tile()
                half = s.const % 2
                return nc.tensor.matmul(psA[bank][:], nT[:, t.const % 2, :],
                                        wqkv_sb[:, what, half * W4:(half + 1) * W4], start=True, stop=True)

            def project_qk(s):
                pe.wait_ge(normT_ready, s.tile().done(2, 2))
                if alive(s - 1):
                    pe.wait_ge(MA_ready, (s - 1).done(1, 2))
                project(s, 0, 0).then_inc(q_done, 1)
                if alive(s - 1):
                    pe.wait_ge(MA_ready, (s - 1).done(2, 2))
                project(s, 1, 1).then_inc(k_done, 1)

            def project_v(s):
                pe.wait_ge(q_ready, s.done())
                project(s, 2, 0).then_inc(v_done, 1)

            def turn_hat(which, bank):
                for h in range(HALF):
                    last = nc.tensor.transpose(psA[bank][:, h * P:(h + 1) * P], hat[:, which, h * P:(h + 1) * P], ident[:])
                return last

            def turn_kq(s):
                pe.wait_ge(hats_ready, s.done(1, 2))
                pe.wait_ge(k_ready, s.done())
                turn_hat(0, 1).then_inc(k_turned, 1)
                pe.wait_ge(hats_ready, s.done(2, 2))
                pe.wait_ge(v_ready, s.done())
                turn_hat(1, 0).then_inc(q_turned, 1)

            def turn_qg(s):
                pe.wait_ge(qg_ready, s.done())
                pe.wait_ge(kT_ready, s.done())
                turn_hat(2, 1).then_inc(qg_turned, 1)

            def decays(s):
                pe.wait_ge(rhsD_ready, s.done())
                pe.wait_ge(qT_ready, s.done())
                nc.tensor.matmul(psA[0][:], after[:], rhsD[:], start=True, stop=False)
                for h in range(HALF):
                    last = nc.tensor.matmul(psA[0][:, h * P:(h + 1) * P], identb[:], below[:], start=False,
                                            stop=h == HALF - 1)
                last.then_inc(D_done, 1)

            def products(s, part):
                if part == 0:
                    pe.wait_ge(kT_ready, s.done())
                    pe.wait_ge(expD_ready, s.done())
                else:
                    pe.wait_ge(qgT_ready, s.done())
                r = s.const % 4
                for j in range(2):
                    h = 2 * part + j
                    last = nc.tensor.matmul(psA[part][:, j * 2 * P:(j + 1) * 2 * P], kqT[:, r, h, 0, :],
                                            kqT[:, r, h, :, :], start=True, stop=True)
                last.then_inc(products_done, 1)

            def inv_first(s):
                pe.wait_ge(W_begun, s.done())
                if alive(s - 1):
                    pe.wait_ge(W_ready, (s - 1).done(NL, NL))
                for h in range(HALF):
                    last = nc.tensor.transpose(psB[0][:, h * P:(h + 1) * P], Wt[:, s.const % 4, h * P:(h + 1) * P], ident[:])
                last.then_inc(T_begun, 1)

            def inv_P(s, l):
                pe.wait_ge(T_ready, s.done(l + 1, NL))
                if l:
                    pe.wait_ge(W_ready, s.done(l, NL))
                else:
                    pe.wait_ge(diagonal_set, s.done())
                for h in range(HALF):
                    last = nc.tensor.matmul(psB[0][:, h * P:(h + 1) * P], MA[:, s.const % 4, h, 0, :],
                                            Tm[:, h * P:(h + 1) * P], start=True, stop=True)
                last.then_inc(P_done, 1)

            def inv_TW(s, l):
                pe.wait_ge(Q_ready, s.done(l + 1, NL))
                r = s.const % 4
                if l < NL - 1:
                    for h in range(HALF):
                        c = slice(h * P, (h + 1) * P)
                        last = nc.tensor.matmul(psB[1][:, c], Wt[:, r, c], Qm[:, c], start=True, stop=True)
                    last.then_inc(T_done, 1)
                for h in range(HALF):
                    c = slice(h * P, (h + 1) * P)
                    last = nc.tensor.matmul(psB[0][:, c], Qm[:, c], Wt[:, r, c], start=True, stop=True)
                last.then_inc(W_done, 1)

            def rec_KS(s):
                if alive(s - 4):
                    pe.wait_ge(S_ready, (s - 4).done())
                if alive(s - 1):
                    pe.wait_ge(OT_ready, (s - 1).done())
                t = s.tile()
                for h in range(HALF):
                    hh = (s.const % 2) * HALF + h
                    last = nc.tensor.matmul(psC[0][:, h * P:(h + 1) * P], kqT[:, s.const % 4, h, 0, :],
                                            S[:, t.const % B, hh, :], start=True, stop=True)
                last.then_inc(KS_done, 1)

            def rec_U(s):
                pe.wait_ge(R_ready, s.done())
                pe.wait_ge(W_ready, s.done(NL, NL))
                if alive(s - 1):
                    pe.wait_ge(S_ready, (s - 1).done())
                for h in range(HALF):
                    c = slice(h * P, (h + 1) * P)
                    last = nc.tensor.matmul(psC[1][:, c], Wt[:, s.const % 4, c], R[:, c], start=True, stop=True)
                last.then_inc(U_done, 1)

            def rec_out(s):
                pe.wait_ge(U_ready, s.done())
                pe.wait_ge(qgT_ready, s.done())
                t, r = s.tile(), s.const % 4
                for h in range(HALF):
                    hh = (s.const % 2) * HALF + h
                    c = slice(h * P, (h + 1) * P)
                    nc.tensor.matmul(psC[0][:, c], S[:, t.const % B, hh, :], qgT[:, r, c], start=True, stop=False)
                    last = nc.tensor.matmul(psC[0][:, c], U[:, c], MA[:, r, h, 1, :], start=False, stop=True)
                last.then_inc(OT_done, 1)
                for h in range(HALF):
                    c = slice(h * P, (h + 1) * P)
                    last = nc.tensor.matmul(psC[1][:, c], kdec[:, r, c], U[:, c], start=True, stop=True)
                last.then_inc(dS_done, 1)

            def expert_in(s, j, up):
                t = s.tile()
                if up:
                    pe.wait_ge(egate_ready, s.done(j + 1, 2))
                elif j:
                    pe.wait_ge(eh_ready, s.done(1, 2))
                elif s.const % 2:
                    if alive(s - 1):
                        pe.wait_ge(ehT_ready, (s - 1).done(2, 2))
                else:
                    if alive(t - 1):
                        pe.wait_ge(branch_ready, (t - 1).done())
                k = 2 * (s.const % 2) + j
                last = nc.tensor.matmul(psM[:], xnT[:, t.const % 2, :], gu_sb[:, up, k * W4:(k + 1) * W4],
                                        start=True, stop=True)
                if up:
                    last.then_inc(eup_done, 1)
                else:
                    last.then_inc(egate_done, 1)

            def expert_T(s, j):
                pe.wait_ge(ehc_ready, s.done(j + 1, 2))
                if j:
                    pe.wait_ge(ehT_ready, s.done(1, 2))
                elif s.const % 2:
                    pe.wait_ge(shh_ready, s.tile().done())
                else:
                    pe.wait_ge(eh_ready, s.done(2, 2))
                for h in range(HALF):
                    last = nc.tensor.transpose(psM[:, h * P:(h + 1) * P], hc[:, j, h * P:(h + 1) * P], ident[:])
                last.then_inc(eh_turned, 1)

            def shared_in(s):
                t = s.tile()
                pe.wait_ge(eh_ready, s.done(2, 2))
                nc.tensor.matmul(psM[:, 0:2 * P], xnT[:, t.const % 2, :], shgu_sb[:].rearrange("p a b -> p (a b)"),
                                     start=True, stop=True).then_inc(shared_done, 1)

            def shared_T(s):
                pe.wait_ge(ehT_ready, s.done(2, 2))
                nc.tensor.transpose(psM[:, 0:P], shh[:], ident[:]).then_inc(shh_turned, 1)

            def experts_down(s):
                pe.wait_ge(shhT_ready, s.tile().done())
                for k in range(KT):
                    nc.tensor.matmul(psM[:, 0:P], hT[:, k, :], down_sb[:, k, :], start=(k == 0), stop=False)
                nc.tensor.matmul(psM[:, 0:P], hT[:, KT, :], shdown_sb[:], start=False, stop=True).then_inc(down_done, 1)

            def fin_x1(t):
                g = t.group(1)
                pe.wait_ge(OT_ready, g.done())
                if alive(t - 1):
                    pe.wait_ge(s_ready, (t - 1).done())
                for h in range(H):
                    gg = (g.const - 1 + h // HALF) % 4
                    c = (h % HALF) * P
                    last = nc.tensor.matmul(psL[:, 256:384], OT[:, gg, c:c + P], wo_sb[:, h, :],
                                            start=(h == 0), stop=(h == H - 1))
                last.then_inc(x1_done, 1)

            def fin_T(t):
                pe.wait_ge(h0_ready, t.done())
                nc.tensor.transpose(psL[:, 384:512], h0[:], ident[:]).then_inc(h0_turned, 1)

            def fin_w1(t, part):
                if part:
                    pe.wait_ge(gelu_ready, t.done(2, FB))
                else:
                    pe.wait_ge(hT_ready, t.done())
                for j in range(2):
                    k = 2 * part + j
                    last = nc.tensor.matmul(psL[:, 256 + j * P:384 + j * P], w1_sb[:, k * P:(k + 1) * P], hT2[:],
                                            start=True, stop=True)
                last.then_inc(w1_done, 1)

            def fin_w2(t):
                pe.wait_ge(gelu_ready, t.done(FB, FB))
                for k in range(FB):
                    last = nc.tensor.matmul(psL[:, 256:384], gel[:, k, :], w2_sb[:, k, :], start=(k == 0),
                                            stop=(k == FB - 1))
                last.then_inc(w2_done, 1)

            def slot(s):
                a = alive(s)
                bs, b = s - 1, alive(s - 1)
                cs, c = s - LAGC, alive(s - LAGC)
                even = s.const % 2 == 0
                f = even and alive(s - LAGF)
                ft = (s - LAGF).tile()
                nxt = (s + 1).tile()
                l = not even and alive(nxt, TILES)
                if a:
                    project_qk(s)
                if b:
                    inv_first(bs)
                if c:
                    rec_KS(cs)
                if a:
                    project_v(s)
                if b:
                    inv_P(bs, 0)
                if a:
                    expert_in(s, 0, 0)
                if b:
                    inv_TW(bs, 0)
                if c:
                    rec_U(cs)
                if b:
                    inv_P(bs, 1)
                if a:
                    expert_in(s, 0, 1)
                    turn_kq(s)
                if b:
                    inv_TW(bs, 1)
                if c:
                    rec_out(cs)
                if b:
                    inv_P(bs, 2)
                if a:
                    expert_in(s, 1, 0)
                    turn_qg(s)
                if b:
                    inv_TW(bs, 2)
                if a:
                    decays(s)
                    expert_in(s, 1, 1)
                if b:
                    inv_P(bs, 3)
                if l:
                    start_T(nxt)
                if f:
                    fin_x1(ft)
                if b:
                    inv_TW(bs, 3)
                if l:
                    start_z(nxt)
                if f:
                    fin_T(ft)
                if a:
                    products(s, 0)
                    products(s, 1)
                if b:
                    inv_P(bs, 4)
                if a and even:
                    expert_T(s, 0)
                if a and not even:
                    shared_in(s)
                if b:
                    inv_TW(bs, 4)
                if l:
                    start_cum(nxt)
                if f:
                    fin_w1(ft, 0)
                if a:
                    if even:
                        expert_T(s, 1)
                    else:
                        expert_T(s, 0)
                if b:
                    inv_P(bs, 5)
                if f:
                    fin_w1(ft, 1)
                if a and not even:
                    expert_T(s, 1)
                if b:
                    inv_TW(bs, 5)
                if a and not even:
                    shared_T(s)
                    experts_down(s)
                if f:
                    fin_w2(ft)

            slots(pe, begin, slot)

        @block.scalar
        def _(act):
            def begin():
                act.wait_ge(weights, n_weights)
                t = Stage(None, RING // 2, 0)
                start_evT(t)
                start_exp(t)
                start_ln(t)
                start_dec(t)

            def start_evT(t):
                act.wait_ge(norm_turned, t.done())
                k = t.const % 2
                if alive(t - 2):
                    act.wait_ge(down_done, (t - 2).done())
                nc.scalar.copy(xnT[:, k, :], psL[:, 0:P]).then_inc(normT_ready, 1)
                nc.scalar.activation(nT[:, k, :], psL[:, P:2 * P], ACT.Identity, bias=ln1_sb[:, 1:2],
                                         scale=ln1_sb[:, 0:1]).then_inc(normT_ready, 1)

            def start_exp(t):
                act.wait_ge(z_ready, t.done(3, 3))
                nc.scalar.activation(ez[:], zm[:], ACT.Exp, scale=-1.0).then_inc(expz_ready, 1)

            def start_ln(t):
                act.wait_ge(sigmoid_ready, t.done(1, 2))
                nc.scalar.activation(lnz[:], ez1[:, H + E:NZ], ACT.Ln).then_inc(logz_ready, 1)

            def start_dec(t):
                act.wait_ge(cum_done, t.done())
                if alive((t - 4).group(1)):
                    act.wait_ge(S_ready, (t - 4).group(1).done())
                nc.scalar.activation(dec[:, n_(t), :], psL[:, NZ + 16:NZ + 16 + 3 * H], ACT.Exp, scale=-1.0).then_inc(decays_ready, 1)

            def silu_qk(s):
                p = s.const % 2
                act.wait_ge(q_done, s.done())
                if alive(s - 2):
                    act.wait_ge(hats_ready, (s - 2).done(2, 2))
                if alive(s - 2):
                    act.wait_ge(qg_ready, (s - 2).done())
                nc.scalar.activation(qk[:, p, 0, :], psA[0][:], ACT.Silu).then_inc(q_ready, 1)
                act.wait_ge(k_done, s.done())
                nc.scalar.activation(qk[:, p, 1, :], psA[1][:], ACT.Silu).then_inc(k_ready, 1)

            def silu_v(s):
                act.wait_ge(v_done, s.done())
                if alive(s - 4):
                    act.wait_ge(R_ready, (s - 4).done())
                nc.scalar.activation(v[:, s.const % 4, :], psA[0][:], ACT.Silu).then_inc(v_ready, 1)

            def copy_kT(s):
                act.wait_ge(k_turned, s.done())
                if alive(s - 4):
                    act.wait_ge(KS_done, (s - 4).done())
                nc.scalar.copy(kqT[:, s.const % 4, :, 0, :], heads(psA[1][:])).then_inc(kT_ready, 1)

            def copy_qgT(s):
                act.wait_ge(qg_turned, s.done())
                if alive(s - 4):
                    act.wait_ge(OT_done, (s - 4).done())
                nc.scalar.copy(heads(qgT[:, s.const % 4, :]), heads(psA[1][:])).then_inc(qgT_ready, 1)

            def exp_D(s):
                act.wait_ge(D_done, s.done())
                if alive(s - 1):
                    act.wait_ge(decay_ready, (s - 1).done())
                nc.scalar.activation(expD[:], psA[0][:], ACT.Exp, scale=-1.0).then_inc(expD_ready, 1)

            def inv_first(s):
                act.wait_ge(T_begun, s.done())
                nc.scalar.copy(Tm[:], psB[0][:]).then_inc(T_ready, 1)

            def inv_TW(s, l):
                act.wait_ge(W_done, s.done(l + 1, NL))
                if l < NL - 1:
                    nc.scalar.copy(Tm[:], psB[1][:]).then_inc(T_ready, 1)
                nc.scalar.copy(Wt[:, s.const % 4, :], psB[0][:]).then_inc(W_ready, 1)

            def rec_U(s):
                act.wait_ge(U_done, s.done())
                if alive(s - 1):
                    act.wait_ge(dS_done, (s - 1).done())
                nc.scalar.mul(U[:], psC[1][:], -1.0).then_inc(U_ready, 1)

            def rec_OT(s):
                act.wait_ge(OT_done, s.done())
                if alive((s - 4).tile()):
                    act.wait_ge(x1_done, (s - 4).tile().done())
                nc.scalar.copy(OT[:, s.const % 4, :], psC[0][:]).then_inc(OT_ready, 1)

            def expert_silu(s, j):
                act.wait_ge(egate_done, s.done(j + 1, 2))
                if alive(s - 1):
                    act.wait_ge(eh_ready, (s - 1).done(j + 1, 2))
                nc.scalar.activation(sgm[:, j, :], psM[:], ACT.Silu).then_inc(egate_ready, 1)

            def shared_silu(s):
                act.wait_ge(shared_done, s.tile().done())
                nc.scalar.activation(shs[:], psM[:, 0:P], ACT.Silu).then_inc(shgate_ready, 1)

            def gate_silu(s):
                t = s.tile()
                act.wait_ge(down_done, t.done())
                if alive(t - 4):
                    act.wait_ge(y_ready, (t - 4).done())
                nc.scalar.activation(gsil[:, n_(t), :], psM[:, 0:P], ACT.Silu).then_inc(branch_ready, 1)

            def fin_gelu(t, part):
                act.wait_ge(w1_done, t.done(part + 1, 2))
                if alive(t - 1):
                    act.wait_ge(w2_done, (t - 1).done())
                for j in range(2):
                    k = 2 * part + j
                    nc.scalar.activation(gel[:, k, :], psL[:, 256 + j * P:384 + j * P], ACT.Gelu,
                                             bias=b1_sb[:, k:k + 1]).then_inc(gelu_ready, 1)

            def slot(s):
                a = alive(s)
                bs, b = s - 1, alive(s - 1)
                cs, c = s - LAGC, alive(s - LAGC)
                even = s.const % 2 == 0
                f = even and alive(s - LAGF)
                ft = (s - LAGF).tile()
                nxt = (s + 1).tile()
                l = not even and alive(nxt, TILES)
                if a:
                    silu_qk(s)
                if b:
                    inv_first(bs)
                if a:
                    silu_v(s)
                    expert_silu(s, 0)
                if b:
                    inv_TW(bs, 0)
                if c:
                    rec_U(cs)
                if a:
                    copy_kT(s)
                if b:
                    inv_TW(bs, 1)
                if c:
                    rec_OT(cs)
                if a:
                    expert_silu(s, 1)
                    copy_qgT(s)
                if b:
                    inv_TW(bs, 2)
                if a:
                    exp_D(s)
                if l:
                    start_evT(nxt)
                if b:
                    inv_TW(bs, 3)
                if l:
                    start_exp(nxt)
                    start_ln(nxt)
                if b:
                    inv_TW(bs, 4)
                if l:
                    start_dec(nxt)
                if a and not even:
                    shared_silu(s)
                if f:
                    fin_gelu(ft, 0)
                    fin_gelu(ft, 1)
                if b:
                    inv_TW(bs, 5)
                if a and not even:
                    gate_silu(s)

            slots(act, begin, slot)

        @block.vector
        def _(dve):
            def begin():
                nc.vector.memset(ones[:], 1.0)
                nc.vector.memset(nhalf[:], -0.5)
                nc.vector.memset(eqa[:], 0.0)
                nc.vector.memset(eqb[:], 0.0)
                nc.vector.memset(eqc[:], 0.0)
                nc.vector.memset(S[:], 0.0)
                dve.wait_ge(weights, n_weights)
                nc.vector.tensor_copy(identb[:], ident[:])
                nc.vector.tensor_scalar(below[:], incl[:], -BIG, BIG, ALU.mult, ALU.add).then_inc(constants_ready, 1)
                dve.wait_ge(constants_ready, 1)
                t = Stage(None, RING // 2, 0)
                start_norm(t)
                start_z(t)
                start_e1(t)
                start_la(t)
                route(t)

            def start_norm(t):
                dve.wait_ge(x_in[n_(t)], t.turn(4).done(16, 16))
                nc.vector.bn_stats(stat[:, 0, :], xin[:, n_(t), :]).then_inc(stats_ready, 1)
                dve.wait_ge(stats_ready, t.done(1, 4))
                dve.sem_inc(passed, 1)
                nc.vector.bn_aggr(mv[:, 0, :], stat[:, 0, :]).then_inc(stats_ready, 1)
                dve.wait_ge(rstd_ready, t.done(2, 4))
                nc.vector.tensor_scalar(xn[:, n_(t), :], xin[:, n_(t), :], mv[:, 0, 0:1], rstd[:, 0, 1:2],
                                            ALU.subtract, ALU.mult).then_inc(normed, 1)
                dve.wait_ge(normed, t.done(1, 2))
                nc.vector.bn_stats(stat[:, 1, :], xn[:, n_(t), :]).then_inc(stats_ready, 1)
                dve.wait_ge(stats_ready, t.done(3, 4))
                dve.sem_inc(passed, 1)
                nc.vector.bn_aggr(mv[:, 1, :], stat[:, 1, :]).then_inc(stats_ready, 1)
                dve.wait_ge(rstd_ready, t.done(4, 4))
                if alive(t - 1):
                    dve.wait_ge(norm_turned, (t - 1).done())
                nc.vector.tensor_scalar(n0[:], xn[:, n_(t), :], mv[:, 1, 0:1], rstd[:, 1, 1:2],
                                            ALU.subtract, ALU.mult).then_inc(normed, 1)

            def start_z(t):
                dve.wait_ge(z_done, t.done())
                nc.vector.tensor_scalar(zm[:, 0:H + E], psL[:, 0:H + E], -80.0, None, ALU.max).then_inc(z_ready, 1)
                nc.vector.tensor_scalar(nz[:], psL[:, H + E:NZ], -1.0, 0.0, ALU.mult, ALU.max).then_inc(z_ready, 1)
                dve.wait_ge(z_ready, t.done(2, 3))
                nc.vector.scalar_tensor_tensor(zm[:, H + E:NZ], nz[:], 2.0, psL[:, H + E:NZ], ALU.mult, ALU.add).then_inc(z_ready, 1)

            def start_e1(t):
                dve.wait_ge(expz_ready, t.done())
                nc.vector.tensor_scalar(ez1[:], ez[:], 1.0, None, ALU.add).then_inc(sigmoid_ready, 1)
                dve.wait_ge(sigmoid_ready, t.done(1, 2))
                if alive((t - 2).group(1)):
                    dve.wait_ge(decay_ready, (t - 2).group(1).done())
                nc.vector.reciprocal(sg[:, t.const % 2, :], ez1[:, 0:H + E]).then_inc(sigmoid_ready, 1)

            def start_la(t):
                dve.wait_ge(logz_ready, t.done())
                if alive((t - 2).group(1)):
                    dve.wait_ge(rhsD_ready, (t - 2).group(1).done())
                nc.vector.tensor_tensor(la[:, t.const % 2, :], lnz[:], nz[:], ALU.add).then_inc(logalpha_ready, 1)

            def route(t):
                k = t.const % 2
                done = [0]

                def step(ins, alone=False):
                    ins.then_inc(routed, 1)
                    done[0] += 1
                    dve.wait_ge(routed, t.done(done[0], 32))
                    if alone:
                        dve.sem_inc(passed, 1)

                def choose(val, thr, k, n, dst):
                    step(nc.vector.tensor_scalar(gt[:, 0:n], val, thr, None, ALU.is_gt))
                    step(nc.vector.tensor_scalar(eq[:, 0:n], val, thr, None, ALU.is_equal))
                    step(nc.vector.tensor_reduce(cnt[:, 0:1], gt[:, 0:n], AX_X, ALU.add))
                    src, a, b = eqc, eqa, eqb
                    step(nc.vector.tensor_scalar(eqc[:, 16:16 + n], val, thr, None, ALU.is_equal))
                    shift = 1
                    while shift < n:
                        step(nc.vector.tensor_tensor(a[:, 16:16 + n], src[:, 16:16 + n],
                                                     src[:, 16 - shift:16 - shift + n], ALU.add))
                        src, a, b = a, b, a
                        shift *= 2
                    step(nc.vector.tensor_scalar(a[:, 16:16 + n], src[:, 16:16 + n], cnt[:, 0:1], k + 0.5,
                                                 ALU.add, ALU.is_lt))
                    step(nc.vector.tensor_tensor(a[:, 16:16 + n], a[:, 16:16 + n], eq[:, 0:n], ALU.mult))
                    step(nc.vector.tensor_tensor(dst, gt[:, 0:n], a[:, 16:16 + n], ALU.add))

                dve.wait_ge(sigmoid_ready, t.done(2, 2))
                step(nc.vector.tensor_tensor(sfc[:], sg[:, k, H:H + E], ecb_sb[:], ALU.add))
                groups = sfc[:].rearrange("p (g e) -> p g e", g=NG)
                step(nc.vector.tensor_reduce(gmx[:], groups, AX_X, ALU.max), alone=True)
                step(nc.vector.max(top[:], gmx[:]))
                choose(gmx[:], top[:, KG - 1:KG], KG, NG, gmask[:])
                step(nc.vector.tensor_tensor(masked[:].rearrange("p (g e) -> p g e", g=NG), groups,
                                             along(gmask[:], EG), ALU.mult), alone=True)
                step(nc.vector.max(top[:], masked[:]))
                choose(masked[:], top[:, TOPK - 1:TOPK], TOPK, E, chosen[:])
                step(nc.vector.tensor_tensor(wsel[:], chosen[:], sg[:, k, H:H + E], ALU.mult))
                step(nc.vector.tensor_reduce(wsum[:, 0:1], wsel[:], AX_X, ALU.add))
                step(nc.vector.tensor_scalar(wsum[:, 0:1], wsum[:, 0:1], 1e-20, None, ALU.add))
                step(nc.vector.reciprocal(wsum[:, 1:2], wsum[:, 0:1]))
                if alive((t - 2).group(1)):
                    dve.wait_ge(ehc_ready, (t - 2).group(1).done(2, 2))
                step(nc.vector.tensor_scalar(comb[:, k, :], wsel[:], wsum[:, 1:2], SCALE, ALU.mult, ALU.mult))
                assert done[0] == 32

            def sums(s):
                dve.wait_ge(squares_ready, s.done(2, 2))
                if alive(s - 1):
                    dve.wait_ge(norms_ready, (s - 1).done(5, 5))
                nc.vector.tensor_reduce(ssq[:], qk2[:].rearrange("p a (h d) -> p (a h) d", h=HALF), AX_X, ALU.add).then_inc(sums_ready, 1)

            def hats(s):
                dve.wait_ge(norms_ready, s.done(2, 5))
                if alive(s - 1):
                    dve.wait_ge(qg_turned, (s - 1).done())
                p = s.const % 2
                nc.vector.tensor_tensor(heads(hat[:, 0, :]), heads(qk[:, p, 1, :]), along(rn[:, 0, HALF:2 * HALF], P),
                                            ALU.mult).then_inc(hats_ready, 1)
                nc.vector.tensor_tensor(heads(hat[:, 1, :]), heads(qk[:, p, 0, :]), along(rn[:, 0, 0:HALF], P),
                                            ALU.mult).then_inc(hats_ready, 1)

            def copy_Tq(s):
                dve.wait_ge(q_turned, s.done())
                nc.vector.tensor_copy(kqT[:, s.const % 4, :, 1, :], heads(psA[0][:])).then_inc(qT_ready, 1)

            def products(s):
                r = s.const % 4
                dve.wait_ge(decay_ready, s.done())
                if alive(s - 4):
                    dve.wait_ge(OT_done, (s - 4).done())
                for part in range(2):
                    dve.wait_ge(products_done, s.done(part + 1, 2))
                    d = decay[:, part * 2 * P:(part + 1) * 2 * P].rearrange("p (h i) -> p h i", h=2)
                    nc.vector.tensor_tensor(
                        MA[:, r, 2 * part:2 * part + 2, :, :],
                        psA[part][:].rearrange("p (h a i) -> p h a i", h=2, a=2),
                        d.unsqueeze(2).to_broadcast([P, 2, 2, P]), ALU.mult).then_inc(MA_ready, 1)

            def inv_Q(s, l):
                dve.wait_ge(P_done, s.done(l + 1, NL))
                if l == 0:
                    if alive(s - 1):
                        dve.wait_ge(W_done, (s - 1).done(NL, NL))
                nc.vector.tensor_tensor(heads(Qm[:]), heads(psB[0][:]), across(level[:, l, :], HALF), ALU.mult).then_inc(Q_ready, 1)

            def rec_R(s):
                dve.wait_ge(KS_done, s.done())
                t = s.tile()
                for h in range(HALF):
                    c = slice(h * P, (h + 1) * P)
                    hh = (s.const % 2) * HALF + h
                    last = nc.vector.scalar_tensor_tensor(R[:, c], psC[0][:, c], dec[:, n_(t), hh:hh + 1],
                                                          v[:, s.const % 4, c], ALU.mult, ALU.subtract)
                last.then_inc(R_ready, 1)

            def rec_S(s):
                dve.wait_ge(dS_done, s.done())
                t = s.tile()
                for h in range(HALF):
                    c = slice(h * P, (h + 1) * P)
                    hh = (s.const % 2) * HALF + h
                    o = 2 * H + hh
                    last = nc.vector.scalar_tensor_tensor(S[:, t.const % B, hh, :], S[:, t.const % B, hh, :],
                                                          dec[:, n_(t), o:o + 1], psC[1][:, c], ALU.mult, ALU.add)
                last.then_inc(S_ready, 1)

            def expert_h(s, j):
                dve.wait_ge(eup_done, s.done(j + 1, 2))
                if alive(s - 1):
                    dve.wait_ge(ehc_ready, (s - 1).done(j + 1, 2))
                nc.vector.tensor_tensor(hm[:, j, :], psM[:], sgm[:, j, :], ALU.mult).then_inc(eh_ready, 1)

            def expert_eT(s, j):
                dve.wait_ge(eh_turned, s.done(j + 1, 2))
                k = (2 * (s.const % 2) + j) * HALF
                nc.vector.tensor_copy(hT[:, k:k + HALF, :], heads(psM[:])).then_inc(ehT_ready, 1)

            def shared_h(s):
                dve.wait_ge(shgate_ready, s.tile().done())
                nc.vector.tensor_tensor(shh[:], psM[:, P:2 * P], shs[:], ALU.mult).then_inc(shh_ready, 1)

            def shared_eT(s):
                dve.wait_ge(shh_turned, s.tile().done())
                nc.vector.tensor_copy(hT[:, KT, :], psM[:, 0:P]).then_inc(shhT_ready, 1)

            def fin_norm(t):
                dve.wait_ge(x1_done, t.done())
                if alive(t - 1):
                    dve.wait_ge(x1b_ready, (t - 1).done())
                nc.vector.tensor_tensor(x1[:], psL[:, 256:384], xn[:, n_(t), :], ALU.add).then_inc(x1_ready, 1)
                dve.wait_ge(x1_ready, t.done())
                nc.vector.bn_stats(stat[:, 2, :], x1[:]).then_inc(x1stats_ready, 1)
                dve.wait_ge(x1stats_ready, t.done(1, 2))
                dve.sem_inc(passed, 1)
                nc.vector.bn_aggr(mv[:, 2, :], stat[:, 2, :]).then_inc(x1stats_ready, 1)

            def fin_h0(t):
                dve.wait_ge(x1rstd_ready, t.done(2, 2))
                nc.vector.tensor_scalar(h0[:], x1[:], mv[:, 2, 0:1], rstd[:, 2, 1:2], ALU.subtract, ALU.mult).then_inc(h0_ready, 1)

            def fin_hT(t):
                dve.wait_ge(h0_turned, t.done())
                nc.vector.tensor_scalar(hT2[:], psL[:, 384:512], ln2_sb[:, 0:1], ln2_sb[:, 1:2], ALU.mult, ALU.add).then_inc(hT_ready, 1)

            def fin_s(t):
                dve.wait_ge(w2_done, t.done())
                dve.wait_ge(x1b_ready, t.done())
                nc.vector.tensor_tensor(fs[:], psL[:, 256:384], x1b[:], ALU.add).then_inc(s_ready, 1)

            def slot(s):
                a = alive(s)
                bs, b = s - 1, alive(s - 1)
                cs, c = s - LAGC, alive(s - LAGC)
                even = s.const % 2 == 0
                f = even and alive(s - LAGF)
                ft = (s - LAGF).tile()
                nxt = (s + 1).tile()
                l = not even and alive(nxt, TILES)
                if c:
                    rec_R(cs)
                if b:
                    inv_Q(bs, 0)
                if a:
                    sums(s)
                if l:
                    start_norm(nxt)
                if a:
                    hats(s)
                if b:
                    inv_Q(bs, 1)
                if a:
                    expert_h(s, 0)
                    copy_Tq(s)
                if b:
                    inv_Q(bs, 2)
                if c:
                    rec_S(cs)
                if a:
                    expert_h(s, 1)
                if b:
                    inv_Q(bs, 3)
                if f:
                    fin_norm(ft)
                if l:
                    start_z(nxt)
                if f:
                    fin_h0(ft)
                    fin_hT(ft)
                if a:
                    products(s)
                if b:
                    inv_Q(bs, 4)
                if l:
                    start_e1(nxt)
                    start_la(nxt)
                if a and even:
                    expert_eT(s, 0)
                if a and not even:
                    shared_h(s)
                if a:
                    if even:
                        expert_eT(s, 1)
                    else:
                        expert_eT(s, 0)
                if b:
                    inv_Q(bs, 5)
                if l:
                    route(nxt)
                if a and not even:
                    expert_eT(s, 1)
                    shared_eT(s)
                if f:
                    fin_s(ft)

            slots(dve, begin, slot)

        @block.gpsimd
        def _(pool):
            def begin():
                pool.wait_ge(weights, n_weights)
                pool.wait_ge(constants_ready, 1)
                t = Stage(None, RING // 2, 0)
                start_rsqrt(t)

            def start_rsqrt(t):
                for k in range(2):
                    pool.wait_ge(stats_ready, t.done(2 * k + 2, 4))
                    pool.sem_inc(passed, 1)
                    nc.gpsimd.tensor_scalar(rstd[:, k, 0:1], mv[:, k, 1:2], EPS, None, ALU.add).then_inc(rstd_ready, 1)
                    pool.wait_ge(rstd_ready, t.done(2 * k + 1, 4))
                    nc.gpsimd.tensor_tensor(rstd[:, k, 1:2], rstd[:, k, 0:1], nhalf[:, 0:1], ALU.pow).then_inc(rstd_ready, 1)

            def fin_rsqrt(t):
                pool.wait_ge(x1stats_ready, t.done(2, 2))
                pool.sem_inc(passed, 1)
                nc.gpsimd.tensor_scalar(rstd[:, 2, 0:1], mv[:, 2, 1:2], EPS, None, ALU.add).then_inc(x1rstd_ready, 1)
                pool.wait_ge(x1rstd_ready, t.done(1, 2))
                nc.gpsimd.tensor_tensor(rstd[:, 2, 1:2], rstd[:, 2, 0:1], nhalf[:, 0:1], ALU.pow).then_inc(x1rstd_ready, 1)

            def squares(s):
                p = s.const % 2
                pool.wait_ge(k_ready, s.done())
                if alive(s - 1):
                    pool.wait_ge(sums_ready, (s - 1).done())
                for w in range(2):
                    nc.gpsimd.tensor_tensor(qk2[:, w, :], qk[:, p, w, :], qk[:, p, w, :], ALU.mult).then_inc(squares_ready, 1)

            def norms(s):
                t = s.tile()
                half = s.const % 2
                hs = slice(half * HALF, (half + 1) * HALF)
                pool.wait_ge(sums_ready, s.done())
                pool.wait_ge(decays_ready, t.done())
                if alive(s - 1):
                    pool.wait_ge(hats_ready, (s - 1).done(2, 2))
                pool.sem_inc(passed, 1)
                nc.gpsimd.tensor_scalar(rn[:, 1, :], ssq[:], L2EPS, None, ALU.add).then_inc(norms_ready, 1)
                pool.wait_ge(norms_ready, s.done(1, 5))
                nc.gpsimd.tensor_tensor(rn[:, 0, :], rn[:, 1, :], nhalf[:], ALU.pow).then_inc(norms_ready, 1)
                pool.wait_ge(norms_ready, s.done(2, 5))
                d = dec[:, n_(t), :]
                nc.gpsimd.tensor_tensor(rn[:, 2, 0:HALF], rn[:, 0, 0:HALF], d[:, hs], ALU.mult).then_inc(norms_ready, 1)
                nc.gpsimd.tensor_tensor(rn[:, 1, 0:HALF], rn[:, 0, HALF:2 * HALF],
                                            d[:, H + half * HALF:H + (half + 1) * HALF], ALU.mult).then_inc(norms_ready, 1)
                pool.wait_ge(norms_ready, s.done(4, 5))
                nc.gpsimd.tensor_tensor(rn[:, 2, HALF:2 * HALF], rn[:, 1, 0:HALF],
                                            sg[:, t.const % 2, hs], ALU.mult).then_inc(norms_ready, 1)
                pool.wait_ge(norms_ready, s.done(5, 5))

            def scale(s):
                p, r = s.const % 2, s.const % 4
                if alive(s - 4):
                    pool.wait_ge(dS_done, (s - 4).done())
                nc.gpsimd.tensor_tensor(heads(kdec[:, r, :]), heads(qk[:, p, 1, :]), along(rn[:, 2, HALF:2 * HALF], P),
                                            ALU.mult).then_inc(kdec_ready, 1)
                if alive(s - 1):
                    pool.wait_ge(qg_turned, (s - 1).done())
                nc.gpsimd.tensor_tensor(heads(hat[:, 2, :]), heads(qk[:, p, 0, :]), along(rn[:, 2, 0:HALF], P),
                                            ALU.mult).then_inc(qg_ready, 1)

            def rhs_D(s):
                t = s.tile()
                half = s.const % 2
                pool.wait_ge(logalpha_ready, t.done())
                if alive(s - 1):
                    pool.wait_ge(D_done, (s - 1).done())
                nc.gpsimd.tensor_tensor(heads(rhsD[:]), across(incl[:], HALF),
                                            along(la[:, t.const % 2, half * HALF:(half + 1) * HALF], P), ALU.mult).then_inc(rhsD_ready, 1)

            def beta_decay(s):
                t = s.tile()
                half = s.const % 2
                pool.wait_ge(expD_ready, s.done())
                if alive(s - 1):
                    pool.wait_ge(MA_ready, (s - 1).done(2, 2))
                nc.gpsimd.tensor_tensor(heads(decay[:]), heads(expD[:]),
                                            along(sg[:, t.const % 2, half * HALF:(half + 1) * HALF], P), ALU.mult).then_inc(decay_ready, 1)

            def diagonal(s):
                m = MA[:, s.const % 4, :, 0, :]
                pool.wait_ge(MA_ready, s.done(2, 2))
                pool.sem_inc(passed, 1)
                nc.gpsimd.affine_select(out=m, in_=m, compare_op=ALU.not_equal, fill=1.0, base=0,
                                            pattern=[[0, HALF], [-1, P]], channel_multiplier=1).then_inc(diagonal_set, 1)

            def inv_first(s):
                pool.wait_ge(diagonal_set, s.done())
                if alive(s - 4):
                    pool.wait_ge(U_done, (s - 4).done())
                nc.gpsimd.tensor_tensor(heads(Wt[:, s.const % 4, :]), MA[:, s.const % 4, :, 0, :],
                                            across(winit[:], HALF), ALU.mult).then_inc(W_begun, 1)

            def expert_c(s, j):
                t = s.tile()
                k = 2 * (s.const % 2) + j
                ne = W4 // I
                pool.wait_ge(eh_ready, s.done(j + 1, 2))
                pool.wait_ge(routed, t.done(32, 32))
                if alive(s - 1):
                    pool.wait_ge(eh_turned, (s - 1).done(j + 1, 2))
                nc.gpsimd.tensor_tensor(hc[:, j, :].rearrange("p (e i) -> p e i", e=ne),
                                            hm[:, j, :].rearrange("p (e i) -> p e i", e=ne),
                                            along(comb[:, t.const % 2, k * ne:(k + 1) * ne], I), ALU.mult).then_inc(ehc_ready, 1)

            def fin_bias(t):
                pool.wait_ge(x1_ready, t.done())
                if alive(t - 1):
                    pool.wait_ge(s_ready, (t - 1).done())
                nc.gpsimd.tensor_tensor(x1b[:], x1[:], b2_sb[:], ALU.add).then_inc(x1b_ready, 1)

            def fin_out(t):
                pool.wait_ge(s_ready, t.done())
                pool.wait_ge(branch_ready, t.done())
                nc.gpsimd.tensor_tensor(fy[:], fs[:], gsil[:, n_(t), :], ALU.mult).then_inc(y_ready, 1)
                pool.wait_ge(y_ready, t.done())
                if alive((t - 2).turn(2)):
                    pool.wait_ge(y_out[t.const % 2], (t - 2).turn(2).done(16, 16))
                nc.gpsimd.tensor_tensor(fo[:, t.const % 2, :], fy[:], xin[:, n_(t), :], ALU.add).then_inc(out_ready, 1)

            def slot(s):
                a = alive(s)
                bs, b = s - 1, alive(s - 1)
                even = s.const % 2 == 0
                f = even and alive(s - LAGF)
                ft = (s - LAGF).tile()
                nxt = (s + 1).tile()
                l = not even and alive(nxt, TILES)
                if b:
                    inv_first(bs)
                if a:
                    squares(s)
                    rhs_D(s)
                if l:
                    start_rsqrt(nxt)
                if a:
                    norms(s)
                    scale(s)
                    expert_c(s, 0)
                    expert_c(s, 1)
                    beta_decay(s)
                if f:
                    fin_rsqrt(ft)
                    fin_bias(ft)
                if a:
                    diagonal(s)
                if f:
                    fin_out(ft)

            slots(pool, begin, slot)


def kernel(**inputs):
    import concourse.bacc as bacc
    from concourse.bass_utils import run_bass_kernel_spmd

    a = {k.replace("L0_attn_", "a_").replace("L0_ffn_", "f_"): np.asarray(v) for k, v in inputs.items()}
    D = a["a_x"].shape[-1]
    H = a["a_Wb"].shape[1]
    F = a["a_W1"].shape[1]
    E, two_i, _ = a["f_experts_gate_up"].shape
    I = two_i // 2
    put = np.ascontiguousarray
    i, j = np.arange(P)[:, None], np.arange(P)[None, :]
    level = np.zeros((P, len(LEVELS), P), np.float32)
    for n, s in enumerate(LEVELS):
        level[:, n, :] = (i == j) * 1.0 - ((i // (2 * s) == j // (2 * s)) & (i // s > j // s))
    arrays = dict(
        x=a["a_x"],
        wqkv=put(np.stack([a["a_Wq"], a["a_Wk"], a["a_Wv"]], 1)),
        wba=put(np.concatenate([a["a_Wb"], a["a_Wa"]], 1)),
        wo=put(a["a_Wo"].reshape(H, P, D).transpose(1, 0, 2)),
        ln1=put(np.stack([a["a_ln1_w"], a["a_ln1_b"]], 1)),
        ln2=put(np.stack([a["a_ln2_w"], a["a_ln2_b"]], 1)),
        w1=a["a_W1"],
        b1=put(a["a_b1"].reshape(F // P, P).T),
        w2=put(a["a_W2"].reshape(F // P, P, D).transpose(1, 0, 2)),
        b2=a["a_b2"],
        gate_t=put(a["f_gate_weight"].T),
        ecb=a["f_e_score_correction_bias"],
        gu=put(a["f_experts_gate_up"].reshape(E, 2, I, D).transpose(3, 1, 0, 2).reshape(D, 2, E * I)),
        down=put(a["f_experts_down"].transpose(0, 2, 1)),
        sh_gu=put(np.stack([a["f_shared_gate_w"].T, a["f_shared_up_w"].T], 1)),
        sh_down=put(a["f_shared_down_w"].T),
        c_ident=np.eye(P, dtype=np.float32),
        c_incl=(i <= j).astype(np.float32),
        c_after=(i > j).astype(np.float32),
        c_level=level,
        c_init=((i == j) * 1.0 - ((i // 2 == j // 2) & (j > i))).astype(np.float32),
    )
    nc = bacc.Bacc("TRN2", target_bir_lowering=False, num_devices=1)
    aps = {k: nc.dram_tensor(f"in_{k}", v.shape, mybir.dt.from_np(v.dtype), kind="ExternalInput").ap()
           for k, v in arrays.items()}
    out = nc.dram_tensor("out_y", a["a_x"].shape, F32, kind="ExternalOutput").ap()
    build(nc, **aps, c_below=None, out=out)
    r = run_bass_kernel_spmd(nc, [{f"in_{k}": v for k, v in arrays.items()}], core_ids=[0])
    return r.results[0]["out_y"]
```

```python
from contextlib import ExitStack

import numpy as np

import concourse.bass as bass
from concourse import mybir

ALU = mybir.AluOpType
ACT = mybir.ActivationFunctionType
F32 = mybir.dt.float32
BF16 = mybir.dt.bfloat16
AX_X = mybir.AxisListType.X

P = 128
HALF = 4
W4 = HALF * P
EPS = 1e-5
L2EPS = 1e-6
BASE = 16
LEVELS = (16, 32, 64)
RING = 8
BIG = 30000.0


class Stage:

    def __init__(self, reg, factor, const):
        self.reg, self.factor, self.const = reg, factor, const

    def __sub__(self, n):
        return Stage(self.reg, self.factor, self.const - n)

    def __add__(self, n):
        return self - (-n)

    def done(self, part=1, of=1):
        c = of * self.const + part
        return c if self.reg is None else self.reg * (of * self.factor) + c

    def group(self, half):
        return Stage(self.reg, 2 * self.factor, 2 * self.const + half)

    def turn(self, n):
        return Stage(self.reg, self.factor // n, self.const // n)

    def tile(self):
        return self.turn(2)


def build(nc, x, wqkv, wba, wo, ln1, ln2, w1, b1, w2, b2, gate_t, ecb, gu, down, sh_gu, sh_down,
          c_ident, c_incl, c_after, c_level, c_eye, out):
    B, T, D = x.shape
    H = wo.shape[1]
    F = w1.shape[1]
    FB = F // P
    E = gate_t.shape[1]
    I = down.shape[1]
    NG, KG, TOPK, SCALE = 8, 4, 6, 2.5
    EG = E // NG
    GB = E * I // W4
    KT = E * I // P
    HALVES = H // HALF
    STEPS = T // P
    TILES = B * STEPS
    GROUPS = TILES * HALVES
    assert D == P and B == 2 and HALVES == 2 and GROUPS % RING == 0
    LAGB = 3
    LAGC = 4
    LAGF = 6
    NK = P // BASE
    NQ = NK * H
    NL = len(LEVELS)

    with ExitStack() as ctx:
        def sb(name, shape, dt=F32):
            return ctx.enter_context(nc.sbuf_tensor(name, shape, dt))

        def ps(name):
            return ctx.enter_context(nc.psum_tensor(name, [P, W4], F32))

        wqkv_sb = sb("wqkv_sb", [P, 3, H * P])
        wba_sb = sb("wba_sb", [P, 2 * H])
        wo_sb = sb("wo_sb", [P, H, P])
        ln1_sb = sb("ln1_sb", [P, 2])
        ln2_sb = sb("ln2_sb", [P, 2])
        w1_sb = sb("w1_sb", [P, F])
        b1_sb = sb("b1_sb", [P, FB])
        w2_sb = sb("w2_sb", [P, FB, P])
        b2_sb = sb("b2_sb", [P, P])
        gate_sb = sb("gate_sb", [P, E])
        ecb_sb = sb("ecb_sb", [P, E])
        gu_sb = sb("gu_sb", [P, 2, E * I])
        down_sb = sb("down_sb", [P, KT, P])
        shgu_sb = sb("shgu_sb", [P, 2, P])
        shdown_sb = sb("shdown_sb", [P, P])
        ident = sb("ident", [P, P])
        incl = sb("incl", [P, P])
        after = sb("after", [P, P])
        level = sb("level", [P, NL, P])
        eye = sb("eye", [NQ, BASE, BASE])
        ones = sb("ones", [P, P])
        nhalf = sb("nhalf", [P, 2 * HALF])
        identb = sb("identb", [P, P], BF16)
        below = sb("below", [P, P], BF16)

        xin = sb("xin", [P, 4, P])
        xres = sb("xres", [P, 2, P])
        xn = sb("xn", [P, 4, P])
        n0 = sb("n0", [P, P])
        stat = sb("stat", [P, 4, 6])
        mv = sb("mv", [P, 4, 2])
        rstd = sb("rstd", [P, 4, 2])
        xnT = sb("xnT", [P, 2, P])
        nT = sb("nT", [P, 2, P])
        NZ = 2 * H + E
        zm = sb("zm", [P, NZ])
        nz = sb("nz", [P, H])
        ez = sb("ez", [P, NZ])
        ez1 = sb("ez1", [P, NZ])
        sg = sb("sg", [P, 2, H + E])
        lnz = sb("lnz", [P, H])
        la = sb("la", [P, 2, H])
        dec = sb("dec", [P, 4, 3 * H])
        sfc = sb("sfc", [P, E])
        gmx = sb("gmx", [P, NG])
        top = sb("top", [P, 8])
        gt = sb("gt", [P, E])
        cnt = sb("cnt", [P, 2])
        eqa = sb("eqa", [P, 16 + E])
        eqb = sb("eqb", [P, 16 + E])
        eqc = sb("eqc", [P, 16 + E])
        eq = sb("eq", [P, E])
        chosen = sb("chosen", [P, E])
        gmask = sb("gmask", [P, NG])
        masked = sb("masked", [P, E])
        wsel = sb("wsel", [P, E])
        wsum = sb("wsum", [P, 2])
        comb = sb("comb", [P, 2, E])
        qk = sb("qk", [P, 2, 2, W4])
        qk2 = sb("qk2", [P, 2, W4])
        ssq = sb("ssq", [P, 2 * HALF])
        rn = sb("rn", [P, 3, 2 * HALF])
        hat = sb("hat", [P, 3, W4])
        v = sb("v", [P, 4, W4])
        kdec = sb("kdec", [P, 4, W4])
        kqT = sb("kqT", [P, 4, HALF, 2, P])
        qgT = sb("qgT", [P, 4, W4])
        rhsD = sb("rhsD", [P, W4])
        expD = sb("expD", [P, W4])
        decay = sb("decay", [P, W4])
        MA = sb("MA", [P, 4, HALF, 2, P])
        blkM = sb("blkM", [NQ, BASE, BASE])
        blkT = sb("blkT", [NQ, 2, BASE, BASE])
        blkP = sb("blkP", [NQ, BASE, BASE])
        base = sb("base", [P, 2, HALVES, HALF, P])
        blocks_dram = nc.dram_tensor("blocks_scratch", (NK, H, BASE, BASE), F32, kind="Internal").ap()
        inverted_dram = nc.dram_tensor("inverted_scratch", (NK, H, 2, BASE, BASE), F32, kind="Internal").ap()
        Wt = sb("Wt", [P, 2, W4])
        Tm = sb("Tm", [P, W4])
        Qm = sb("Qm", [P, W4])
        S = sb("S", [P, B, H, P])
        R = sb("R", [P, W4])
        U = sb("U", [P, W4])
        OT = sb("OT", [P, 4, W4])
        sgm = sb("sgm", [P, 2, W4])
        hT = sb("hT", [P, KT + 1, P])
        shs = sb("shs", [P, P])
        shh = sb("shh", [P, P])
        gsil = sb("gsil", [P, 4, P])
        x1 = sb("x1", [P, P])
        x1b = sb("x1b", [P, P])
        h0 = sb("h0", [P, P])
        hT2 = sb("hT2", [P, P])
        gel = sb("gel", [P, FB, P])
        fs = sb("fs", [P, P])
        fy = sb("fy", [P, P])
        fo = sb("fo", [P, 2, P])

        psA = [ps("psA0"), ps("psA1")]
        psB = [ps("psB0"), ps("psB1")]
        psC = [ps("psC0"), ps("psC1")]
        psM = ps("psM")
        psL = ps("psL")

        def sem(name):
            return ctx.enter_context(nc.semaphore(name))

        weights = sem("weights")
        constants_ready = sem("constants_ready")
        passed = sem("passed")
        stats_ready = sem("stats_ready")
        rstd_ready = sem("rstd_ready")
        normed = sem("normed")
        norm_turned = sem("norm_turned")
        normT_ready = sem("normT_ready")
        z_done = sem("z_done")
        z_ready = sem("z_ready")
        expz_ready = sem("expz_ready")
        sigmoid_ready = sem("sigmoid_ready")
        logz_ready = sem("logz_ready")
        logalpha_ready = sem("logalpha_ready")
        cum_done = sem("cum_done")
        decays_ready = sem("decays_ready")
        routed = sem("routed")
        q_done = sem("q_done")
        k_done = sem("k_done")
        v_done = sem("v_done")
        q_ready = sem("q_ready")
        k_ready = sem("k_ready")
        v_ready = sem("v_ready")
        squares_ready = sem("squares_ready")
        sums_ready = sem("sums_ready")
        norms_ready = sem("norms_ready")
        hats_ready = sem("hats_ready")
        kdec_ready = sem("kdec_ready")
        qg_ready = sem("qg_ready")
        k_turned = sem("k_turned")
        q_turned = sem("q_turned")
        qg_turned = sem("qg_turned")
        kT_ready = sem("kT_ready")
        qT_ready = sem("qT_ready")
        qgT_ready = sem("qgT_ready")
        rhsD_ready = sem("rhsD_ready")
        D_done = sem("D_done")
        expD_ready = sem("expD_ready")
        decay_ready = sem("decay_ready")
        products_done = sem("products_done")
        MA_ready = sem("MA_ready")
        diagonal_set = sem("diagonal_set")
        P_done = sem("P_done")
        Q_ready = sem("Q_ready")
        T_done = sem("T_done")
        W_done = sem("W_done")
        T_ready = sem("T_ready")
        W_ready = sem("W_ready")
        blocks_out = sem("blocks_out")
        blocks_in = sem("blocks_in")
        block_steps = sem("block_steps")
        inverted_out = sem("inverted_out")
        base_ready = sem("base_ready")
        x_again = [sem(f"x_again{k}") for k in range(2)]
        KS_done = sem("KS_done")
        R_ready = sem("R_ready")
        U_done = sem("U_done")
        U_ready = sem("U_ready")
        OT_done = sem("OT_done")
        dS_done = sem("dS_done")
        OT_ready = sem("OT_ready")
        S_ready = sem("S_ready")
        egate_done = sem("egate_done")
        egate_ready = sem("egate_ready")
        eup_done = sem("eup_done")
        eh_ready = sem("eh_ready")
        ehc_ready = sem("ehc_ready")
        eh_turned = sem("eh_turned")
        ehT_ready = sem("ehT_ready")
        shared_done = sem("shared_done")
        shgate_ready = sem("shgate_ready")
        shh_ready = sem("shh_ready")
        shh_turned = sem("shh_turned")
        shhT_ready = sem("shhT_ready")
        down_done = sem("down_done")
        branch_ready = sem("branch_ready")
        x1_done = sem("x1_done")
        x1_ready = sem("x1_ready")
        x1stats_ready = sem("x1stats_ready")
        x1rstd_ready = sem("x1rstd_ready")
        h0_ready = sem("h0_ready")
        x1b_ready = sem("x1b_ready")
        h0_turned = sem("h0_turned")
        hT_ready = sem("hT_ready")
        w1_done = sem("w1_done")
        gelu_ready = sem("gelu_ready")
        w2_done = sem("w2_done")
        s_ready = sem("s_ready")
        y_ready = sem("y_ready")
        out_ready = sem("out_ready")
        x_in = [sem(f"x_in{k}") for k in range(4)]
        y_out = [sem(f"y_out{k}") for k in range(2)]

        def heads(t, n=HALF):
            return t.rearrange("p (h d) -> p h d", h=n)

        def along(t, n):
            return t.unsqueeze(2).to_broadcast([P, t.shape[1], n])

        def across(t, n):
            return t.unsqueeze(1).to_broadcast([P, n, t.shape[1]])

        loads = [(wqkv_sb, wqkv), (wba_sb, wba), (wo_sb, wo), (ln1_sb, ln1), (ln2_sb, ln2), (w1_sb, w1), (b1_sb, b1),
                 (w2_sb, w2), (gate_sb, gate_t), (gu_sb, gu), (shgu_sb, sh_gu),
                 (shdown_sb, sh_down), (ident, c_ident), (incl, c_incl), (after, c_after), (level, c_level),
                 (eye, c_eye)]

        def n_(t):
            return t.const % 4

        block = ctx.enter_context(nc.Block())

        def slots(eng, begin, slot):
            nc.disable_value_cache = True
            begin()
            for c in range(RING):
                slot(Stage(None, RING, c))
            with eng.Fori(1, GROUPS // RING - 1) as i:
                for c in range(RING):
                    slot(Stage(i, RING, c))
            for c in range(GROUPS - RING, GROUPS + LAGF + 3):
                slot(Stage(None, RING, c))

        def alive(st, total=GROUPS):
            return st.reg is not None or 0 <= st.const < total

        @block.sync
        def _(sp):
            for dst, src in loads:
                sp.dma_start(dst[:], src).then_inc(weights, 16)
            sp.dma_start(down_sb[:], down.rearrange("(k q) i h -> (q i) k h", q=2)).then_inc(weights, 16)
            sp.dma_start(b2_sb[:], b2.partition_broadcast(P)).then_inc(weights, 16)
            sp.dma_start(ecb_sb[:], ecb.partition_broadcast(P)).then_inc(weights, 16)

            def rows(t):
                step = (t.const // B) * P
                return slice(step, step + P) if t.reg is None else bass.ds(t.reg * (t.factor // B * P) + step, P)

            def load(t):
                if alive(t - 4):
                    sp.wait_ge(normed, (t - 4).done(1, 2))
                sp.dma_start(xin[:, n_(t), :], x[t.const % B, rows(t), :]).then_inc(x_in[n_(t)], 16)

            def load_again(t):
                if alive(t - 2):
                    sp.wait_ge(out_ready, (t - 2).done())
                sp.dma_start(xres[:, t.const % 2, :], x[t.const % B, rows(t), :]).then_inc(x_again[t.const % 2], 16)

            def store(t):
                sp.wait_ge(out_ready, t.done())
                sp.dma_start(out[t.const % B, rows(t), :], fo[:, t.const % 2, :]).then_inc(y_out[t.const % 2], 16)

            def blocks_to_partitions(t):
                sp.wait_ge(diagonal_set, t.group(1).done())
                r = t.group(0).const % 4
                for k in range(NK):
                    c = slice(k * BASE, (k + 1) * BASE)
                    sp.dma_start(blocks_dram[k].rearrange("h j i -> j h i"),
                                 MA[c, r:r + 2, :, 0, c].rearrange("j g h i -> j (g h) i")).then_inc(blocks_out, 16)
                sp.wait_ge(blocks_out, t.done(16 * NK, 16 * NK))
                sp.dma_start(blkM[:].rearrange("q j i -> q (j i)"),
                             blocks_dram.rearrange("k h j i -> (k h) (j i)")).then_inc(blocks_in, 16)

            def inverses_in_place(t):
                sp.wait_ge(block_steps, t.done(2 * BASE, 2 * BASE))
                sp.dma_start(inverted_dram.rearrange("k h a j i -> (k h) (a j i)"),
                             blkT[:].rearrange("q a j i -> q (a j i)")).then_inc(inverted_out, 16)
                sp.wait_ge(inverted_out, t.done(16, 16))
                if alive(t - 1):
                    sp.wait_ge(W_done, (t - 1).group(1).done(1, NL))
                for k in range(NK):
                    c = slice(k * BASE, (k + 1) * BASE)
                    for a in range(2):
                        sp.dma_start(base[c, a, :, :, c].rearrange("j g h i -> j (g h) i"),
                                     inverted_dram[k, :, a].rearrange("h j i -> j h i")).then_inc(base_ready, 16)

            def begin():
                for k in range(4):
                    load(Stage(None, RING // 2, k))
                load_again(Stage(None, RING // 2, 0))

            def slot(s):
                even = s.const % 2 == 0
                if not even:
                    x_tile = (s + 1).tile() + 3
                    if alive(x_tile, TILES) and alive(s):
                        load(x_tile)
                    return
                tile = (s - 2).tile()
                if alive(tile, TILES):
                    blocks_to_partitions(tile)
                ft = (s - LAGF).tile()
                if alive(ft + 1, TILES) and alive(ft, TILES):
                    load_again(ft + 1)
                if alive(ft - 1, TILES):
                    store(ft - 1)
                if alive(tile, TILES):
                    inverses_in_place(tile)

            slots(sp, begin, slot)
            for k in range(2):
                sp.wait_ge(y_out[k], 16 * TILES // 2)

        n_weights = 16 * (len(loads) + 3)

        @block.tensor
        def _(pe):
            def begin():
                pe.wait_ge(weights, n_weights)
                pe.wait_ge(constants_ready, 1)
                start_T(Stage(None, RING // 2, 0))
                start_z(Stage(None, RING // 2, 0))
                start_cum(Stage(None, RING // 2, 0))

            def start_T(t):
                pe.wait_ge(normed, t.done(2, 2))
                if alive(t - 1):
                    pe.wait_ge(decays_ready, (t - 1).done())
                nc.tensor.transpose(psL[:, 0:P], xn[:, n_(t), :], ident[:])
                nc.tensor.transpose(psL[:, P:2 * P], n0[:], ident[:]).then_inc(norm_turned, 1)

            def start_z(t):
                pe.wait_ge(normT_ready, t.done(2, 2))
                k = t.const % 2
                nc.tensor.matmul(psL[:, 0:H], nT[:, k, :], wba_sb[:, 0:H], start=True, stop=True)
                nc.tensor.matmul(psL[:, H + E:NZ], nT[:, k, :], wba_sb[:, H:2 * H], start=True, stop=True)
                nc.tensor.matmul(psL[:, H:H + E], xnT[:, k, :], gate_sb[:], start=True, stop=True).then_inc(z_done, 1)

            def start_cum(t):
                pe.wait_ge(logalpha_ready, t.done())
                k = t.const % 2
                for j, m in enumerate((incl, after, ones)):
                    o = NZ + 16 + j * H
                    last = nc.tensor.matmul(psL[:, o:o + H], m[:], la[:, k, :], start=True, stop=True)
                last.then_inc(cum_done, 1)

            def project(s, what, bank):
                t = s.tile()
                half = s.const % 2
                return nc.tensor.matmul(psA[bank][:], nT[:, t.const % 2, :],
                                        wqkv_sb[:, what, half * W4:(half + 1) * W4], start=True, stop=True)

            def project_qk(s):
                pe.wait_ge(normT_ready, s.tile().done(2, 2))
                if alive(s - 1):
                    pe.wait_ge(MA_ready, (s - 1).done(1, 2))
                project(s, 0, 0).then_inc(q_done, 1)
                if alive(s - 1):
                    pe.wait_ge(MA_ready, (s - 1).done(2, 2))
                project(s, 1, 1).then_inc(k_done, 1)

            def project_v(s):
                pe.wait_ge(q_ready, s.done())
                project(s, 2, 0).then_inc(v_done, 1)

            def turn_hat(which, bank):
                for h in range(HALF):
                    last = nc.tensor.transpose(psA[bank][:, h * P:(h + 1) * P], hat[:, which, h * P:(h + 1) * P], ident[:])
                return last

            def turn_kq(s):
                pe.wait_ge(hats_ready, s.done(1, 2))
                pe.wait_ge(k_ready, s.done())
                turn_hat(0, 1).then_inc(k_turned, 1)
                pe.wait_ge(hats_ready, s.done(2, 2))
                pe.wait_ge(v_ready, s.done())
                turn_hat(1, 0).then_inc(q_turned, 1)

            def turn_qg(s):
                pe.wait_ge(qg_ready, s.done())
                pe.wait_ge(kT_ready, s.done())
                turn_hat(2, 1).then_inc(qg_turned, 1)

            def decays(s):
                pe.wait_ge(rhsD_ready, s.done())
                pe.wait_ge(qT_ready, s.done())
                nc.tensor.matmul(psA[0][:], after[:], rhsD[:], start=True, stop=False)
                for h in range(HALF):
                    last = nc.tensor.matmul(psA[0][:, h * P:(h + 1) * P], identb[:], below[:], start=False,
                                            stop=h == HALF - 1)
                last.then_inc(D_done, 1)

            def products(s, part):
                if part == 0:
                    pe.wait_ge(kT_ready, s.done())
                    pe.wait_ge(expD_ready, s.done())
                else:
                    pe.wait_ge(qgT_ready, s.done())
                r = s.const % 4
                for j in range(2):
                    h = 2 * part + j
                    last = nc.tensor.matmul(psA[part][:, j * 2 * P:(j + 1) * 2 * P], kqT[:, r, h, 0, :],
                                            kqT[:, r, h, :, :], start=True, stop=True)
                last.then_inc(products_done, 1)

            def inv_P(s, l):
                if l:
                    pe.wait_ge(T_ready, s.done(l, NL - 1))
                    pe.wait_ge(W_ready, s.done(l, NL))
                else:
                    pe.wait_ge(base_ready, s.tile().done(32 * NK, 32 * NK))
                    if alive(s - 1):
                        pe.wait_ge(W_ready, (s - 1).done(NL, NL))
                for h in range(HALF):
                    c = slice(h * P, (h + 1) * P)
                    T = Tm[:, c] if l else base[:, 0, s.const % 2, h, :]
                    last = nc.tensor.matmul(psB[0][:, c], MA[:, s.const % 4, h, 0, :], T, start=True, stop=True)
                last.then_inc(P_done, 1)

            def inv_TW(s, l):
                pe.wait_ge(Q_ready, s.done(l + 1, NL))
                W = [Wt[:, s.const % 2, h * P:(h + 1) * P] if l else base[:, 1, s.const % 2, h, :] for h in range(HALF)]
                if l < NL - 1:
                    for h in range(HALF):
                        c = slice(h * P, (h + 1) * P)
                        last = nc.tensor.matmul(psB[1][:, c], W[h], Qm[:, c], start=True, stop=True)
                    last.then_inc(T_done, 1)
                for h in range(HALF):
                    c = slice(h * P, (h + 1) * P)
                    last = nc.tensor.matmul(psB[0][:, c], Qm[:, c], W[h], start=True, stop=True)
                last.then_inc(W_done, 1)

            def rec_KS(s):
                if alive(s - 4):
                    pe.wait_ge(S_ready, (s - 4).done())
                if alive(s - 1):
                    pe.wait_ge(OT_ready, (s - 1).done())
                t = s.tile()
                for h in range(HALF):
                    hh = (s.const % 2) * HALF + h
                    last = nc.tensor.matmul(psC[0][:, h * P:(h + 1) * P], kqT[:, s.const % 4, h, 0, :],
                                            S[:, t.const % B, hh, :], start=True, stop=True)
                last.then_inc(KS_done, 1)

            def rec_U(s):
                pe.wait_ge(R_ready, s.done())
                pe.wait_ge(W_ready, s.done(NL, NL))
                if alive(s - 1):
                    pe.wait_ge(S_ready, (s - 1).done())
                for h in range(HALF):
                    c = slice(h * P, (h + 1) * P)
                    last = nc.tensor.matmul(psC[1][:, c], Wt[:, s.const % 2, c], R[:, c], start=True, stop=True)
                last.then_inc(U_done, 1)

            def rec_out(s):
                pe.wait_ge(U_ready, s.done())
                pe.wait_ge(qgT_ready, s.done())
                t, r = s.tile(), s.const % 4
                for h in range(HALF):
                    hh = (s.const % 2) * HALF + h
                    c = slice(h * P, (h + 1) * P)
                    nc.tensor.matmul(psC[0][:, c], S[:, t.const % B, hh, :], qgT[:, r, c], start=True, stop=False)
                    last = nc.tensor.matmul(psC[0][:, c], U[:, c], MA[:, r, h, 1, :], start=False, stop=True)
                last.then_inc(OT_done, 1)
                for h in range(HALF):
                    c = slice(h * P, (h + 1) * P)
                    last = nc.tensor.matmul(psC[1][:, c], kdec[:, r, c], U[:, c], start=True, stop=True)
                last.then_inc(dS_done, 1)

            def expert_in(s, j, up):
                t = s.tile()
                if up:
                    pe.wait_ge(egate_ready, s.done(j + 1, 2))
                elif j:
                    pe.wait_ge(eh_ready, s.done(1, 2))
                elif s.const % 2:
                    if alive(s - 1):
                        pe.wait_ge(ehT_ready, (s - 1).done(2, 2))
                else:
                    if alive(t - 1):
                        pe.wait_ge(branch_ready, (t - 1).done())
                k = 2 * (s.const % 2) + j
                last = nc.tensor.matmul(psM[:], xnT[:, t.const % 2, :], gu_sb[:, up, k * W4:(k + 1) * W4],
                                        start=True, stop=True)
                if up:
                    last.then_inc(eup_done, 1)
                else:
                    last.then_inc(egate_done, 1)

            def expert_T(s, j):
                pe.wait_ge(ehc_ready, s.done(j + 1, 2))
                if j:
                    pe.wait_ge(ehT_ready, s.done(1, 2))
                elif s.const % 2:
                    pe.wait_ge(shh_ready, s.tile().done())
                else:
                    pe.wait_ge(eh_ready, s.done(2, 2))
                for h in range(HALF):
                    last = nc.tensor.transpose(psM[:, h * P:(h + 1) * P], sgm[:, j, h * P:(h + 1) * P], ident[:])
                last.then_inc(eh_turned, 1)

            def shared_in(s):
                t = s.tile()
                pe.wait_ge(eh_ready, s.done(2, 2))
                nc.tensor.matmul(psM[:, 0:2 * P], xnT[:, t.const % 2, :], shgu_sb[:].rearrange("p a b -> p (a b)"),
                                     start=True, stop=True).then_inc(shared_done, 1)

            def shared_T(s):
                pe.wait_ge(ehT_ready, s.done(2, 2))
                nc.tensor.transpose(psM[:, 0:P], shh[:], ident[:]).then_inc(shh_turned, 1)

            def experts_down(s):
                pe.wait_ge(shhT_ready, s.tile().done())
                for k in range(KT):
                    nc.tensor.matmul(psM[:, 0:P], hT[:, k, :], down_sb[:, k, :], start=(k == 0), stop=False)
                nc.tensor.matmul(psM[:, 0:P], hT[:, KT, :], shdown_sb[:], start=False, stop=True).then_inc(down_done, 1)

            def fin_x1(t):
                g = t.group(1)
                pe.wait_ge(OT_ready, g.done())
                if alive(t - 1):
                    pe.wait_ge(s_ready, (t - 1).done())
                for h in range(H):
                    gg = (g.const - 1 + h // HALF) % 4
                    c = (h % HALF) * P
                    last = nc.tensor.matmul(psL[:, 256:384], OT[:, gg, c:c + P], wo_sb[:, h, :],
                                            start=(h == 0), stop=(h == H - 1))
                last.then_inc(x1_done, 1)

            def fin_T(t):
                pe.wait_ge(h0_ready, t.done())
                nc.tensor.transpose(psL[:, 384:512], h0[:], ident[:]).then_inc(h0_turned, 1)

            def fin_w1(t, part):
                if part:
                    pe.wait_ge(gelu_ready, t.done(2, FB))
                else:
                    pe.wait_ge(hT_ready, t.done())
                for j in range(2):
                    k = 2 * part + j
                    last = nc.tensor.matmul(psL[:, 256 + j * P:384 + j * P], w1_sb[:, k * P:(k + 1) * P], hT2[:],
                                            start=True, stop=True)
                last.then_inc(w1_done, 1)

            def fin_w2(t):
                pe.wait_ge(gelu_ready, t.done(FB, FB))
                for k in range(FB):
                    last = nc.tensor.matmul(psL[:, 256:384], gel[:, k, :], w2_sb[:, k, :], start=(k == 0),
                                            stop=(k == FB - 1))
                last.then_inc(w2_done, 1)

            def slot(s):
                a = alive(s)
                bs, b = s - LAGB, alive(s - LAGB)
                cs, c = s - LAGC, alive(s - LAGC)
                even = s.const % 2 == 0
                f = even and alive(s - LAGF)
                ft = (s - LAGF).tile()
                nxt = (s + 1).tile()
                l = not even and alive(nxt, TILES)
                if a:
                    project_qk(s)
                if c:
                    rec_KS(cs)
                if f:
                    fin_x1(ft)
                if a:
                    project_v(s)
                if b:
                    inv_P(bs, 0)
                if a:
                    expert_in(s, 0, 0)
                if b:
                    inv_TW(bs, 0)
                if c:
                    rec_U(cs)
                if l:
                    start_T(nxt)
                if f:
                    fin_T(ft)
                if b:
                    inv_P(bs, 1)
                if a:
                    expert_in(s, 0, 1)
                    turn_kq(s)
                if b:
                    inv_TW(bs, 1)
                if c:
                    rec_out(cs)
                if f:
                    fin_w1(ft, 0)
                if l:
                    start_z(nxt)
                if b:
                    inv_P(bs, 2)
                if a:
                    expert_in(s, 1, 0)
                    turn_qg(s)
                if b:
                    inv_TW(bs, 2)
                if a:
                    decays(s)
                if f:
                    fin_w1(ft, 1)
                if l:
                    start_cum(nxt)
                if a:
                    expert_in(s, 1, 1)
                    if even:
                        expert_T(s, 0)
                    else:
                        shared_in(s)
                    products(s, 0)
                    products(s, 1)
                    if even:
                        expert_T(s, 1)
                    else:
                        expert_T(s, 0)
                        expert_T(s, 1)
                        shared_T(s)
                        experts_down(s)
                if f:
                    fin_w2(ft)

            slots(pe, begin, slot)

        @block.scalar
        def _(act):
            def begin():
                act.wait_ge(weights, n_weights)
                t = Stage(None, RING // 2, 0)
                start_evT(t)
                start_exp(t)
                start_ln(t)
                start_dec(t)

            def start_evT(t):
                act.wait_ge(norm_turned, t.done())
                k = t.const % 2
                if alive(t - 2):
                    act.wait_ge(down_done, (t - 2).done())
                nc.scalar.copy(xnT[:, k, :], psL[:, 0:P]).then_inc(normT_ready, 1)
                nc.scalar.activation(nT[:, k, :], psL[:, P:2 * P], ACT.Identity, bias=ln1_sb[:, 1:2],
                                         scale=ln1_sb[:, 0:1]).then_inc(normT_ready, 1)

            def start_exp(t):
                act.wait_ge(z_ready, t.done(3, 3))
                nc.scalar.activation(ez[:], zm[:], ACT.Exp, scale=-1.0).then_inc(expz_ready, 1)

            def start_ln(t):
                act.wait_ge(sigmoid_ready, t.done(1, 2))
                nc.scalar.activation(lnz[:], ez1[:, H + E:NZ], ACT.Ln).then_inc(logz_ready, 1)

            def start_dec(t):
                act.wait_ge(cum_done, t.done())
                if alive((t - 4).group(1)):
                    act.wait_ge(S_ready, (t - 4).group(1).done())
                nc.scalar.activation(dec[:, n_(t), :], psL[:, NZ + 16:NZ + 16 + 3 * H], ACT.Exp, scale=-1.0).then_inc(decays_ready, 1)

            def silu_qk(s):
                p = s.const % 2
                act.wait_ge(q_done, s.done())
                if alive(s - 2):
                    act.wait_ge(hats_ready, (s - 2).done(2, 2))
                if alive(s - 2):
                    act.wait_ge(qg_ready, (s - 2).done())
                nc.scalar.activation(qk[:, p, 0, :], psA[0][:], ACT.Silu).then_inc(q_ready, 1)
                act.wait_ge(k_done, s.done())
                nc.scalar.activation(qk[:, p, 1, :], psA[1][:], ACT.Silu).then_inc(k_ready, 1)

            def silu_v(s):
                act.wait_ge(v_done, s.done())
                if alive(s - 4):
                    act.wait_ge(R_ready, (s - 4).done())
                nc.scalar.activation(v[:, s.const % 4, :], psA[0][:], ACT.Silu).then_inc(v_ready, 1)

            def copy_kT(s):
                act.wait_ge(k_turned, s.done())
                if alive(s - 4):
                    act.wait_ge(KS_done, (s - 4).done())
                nc.scalar.copy(kqT[:, s.const % 4, :, 0, :], heads(psA[1][:])).then_inc(kT_ready, 1)

            def copy_qgT(s):
                act.wait_ge(qg_turned, s.done())
                if alive(s - 4):
                    act.wait_ge(OT_done, (s - 4).done())
                nc.scalar.copy(heads(qgT[:, s.const % 4, :]), heads(psA[1][:])).then_inc(qgT_ready, 1)

            def exp_D(s):
                act.wait_ge(D_done, s.done())
                if alive(s - 1):
                    act.wait_ge(decay_ready, (s - 1).done())
                nc.scalar.activation(expD[:], psA[0][:], ACT.Exp, scale=-1.0).then_inc(expD_ready, 1)

            def inv_TW(s, l):
                act.wait_ge(W_done, s.done(l + 1, NL))
                if l < NL - 1:
                    nc.scalar.copy(Tm[:], psB[1][:]).then_inc(T_ready, 1)
                nc.scalar.copy(Wt[:, s.const % 2, :], psB[0][:]).then_inc(W_ready, 1)

            def rec_U(s):
                act.wait_ge(U_done, s.done())
                if alive(s - 1):
                    act.wait_ge(dS_done, (s - 1).done())
                nc.scalar.mul(U[:], psC[1][:], -1.0).then_inc(U_ready, 1)

            def rec_OT(s):
                act.wait_ge(OT_done, s.done())
                if alive((s - 4).tile()):
                    act.wait_ge(x1_done, (s - 4).tile().done())
                nc.scalar.copy(OT[:, s.const % 4, :], psC[0][:]).then_inc(OT_ready, 1)

            def expert_silu(s, j):
                act.wait_ge(egate_done, s.done(j + 1, 2))
                if alive(s - 1):
                    act.wait_ge(eh_turned, (s - 1).done(j + 1, 2))
                nc.scalar.activation(sgm[:, j, :], psM[:], ACT.Silu).then_inc(egate_ready, 1)

            def shared_silu(s):
                act.wait_ge(shared_done, s.tile().done())
                nc.scalar.activation(shs[:], psM[:, 0:P], ACT.Silu).then_inc(shgate_ready, 1)

            def gate_silu(s):
                t = s.tile()
                act.wait_ge(down_done, t.done())
                if alive(t - 4):
                    act.wait_ge(y_ready, (t - 4).done())
                nc.scalar.activation(gsil[:, n_(t), :], psM[:, 0:P], ACT.Silu).then_inc(branch_ready, 1)

            def fin_gelu(t, part):
                act.wait_ge(w1_done, t.done(part + 1, 2))
                if alive(t - 1):
                    act.wait_ge(w2_done, (t - 1).done())
                for j in range(2):
                    k = 2 * part + j
                    nc.scalar.activation(gel[:, k, :], psL[:, 256 + j * P:384 + j * P], ACT.Gelu,
                                             bias=b1_sb[:, k:k + 1]).then_inc(gelu_ready, 1)

            def slot(s):
                a = alive(s)
                bs, b = s - LAGB, alive(s - LAGB)
                cs, c = s - LAGC, alive(s - LAGC)
                even = s.const % 2 == 0
                f = even and alive(s - LAGF)
                ft = (s - LAGF).tile()
                nxt = (s + 1).tile()
                l = not even and alive(nxt, TILES)
                if a:
                    silu_qk(s)
                    silu_v(s)
                    expert_silu(s, 0)
                if b:
                    inv_TW(bs, 0)
                if c:
                    rec_U(cs)
                if l:
                    start_evT(nxt)
                if a:
                    copy_kT(s)
                if b:
                    inv_TW(bs, 1)
                if c:
                    rec_OT(cs)
                if a:
                    expert_silu(s, 1)
                    copy_qgT(s)
                if f:
                    fin_gelu(ft, 0)
                if b:
                    inv_TW(bs, 2)
                if l:
                    start_exp(nxt)
                if a:
                    exp_D(s)
                if l:
                    start_ln(nxt)
                    start_dec(nxt)
                if f:
                    fin_gelu(ft, 1)
                if a and not even:
                    shared_silu(s)
                    gate_silu(s)

            slots(act, begin, slot)

        @block.vector
        def _(dve):
            def begin():
                nc.vector.memset(ones[:], 1.0)
                nc.vector.memset(nhalf[:], -0.5)
                nc.vector.memset(eqa[:], 0.0)
                nc.vector.memset(eqb[:], 0.0)
                nc.vector.memset(eqc[:], 0.0)
                nc.vector.memset(S[:], 0.0)
                nc.vector.memset(base[:].rearrange("p a g h i -> p (a g h i)"), 0.0)
                dve.wait_ge(weights, n_weights)
                nc.vector.tensor_copy(identb[:], ident[:])
                nc.vector.tensor_scalar(below[:], incl[:], -BIG, BIG, ALU.mult, ALU.add).then_inc(constants_ready, 1)
                dve.wait_ge(constants_ready, 1)
                t = Stage(None, RING // 2, 0)
                norm_stats(t)
                norm_input(t)
                norm_branch(t)
                start_z(t)
                start_e1(t)
                start_la(t)
                route(t)

            def norm_stats(t):
                dve.wait_ge(x_in[n_(t)], t.turn(4).done(16, 16))
                nc.vector.bn_stats(stat[:, 0, :], xin[:, n_(t), :]).then_inc(stats_ready, 1)
                dve.wait_ge(stats_ready, t.done(1, 4))
                dve.sem_inc(passed, 1)
                nc.vector.bn_aggr(mv[:, 0, :], stat[:, 0, :]).then_inc(stats_ready, 1)

            def norm_input(t):
                dve.wait_ge(rstd_ready, t.done(2, 4))
                nc.vector.tensor_scalar(xn[:, n_(t), :], xin[:, n_(t), :], mv[:, 0, 0:1], rstd[:, 0, 1:2],
                                        ALU.subtract, ALU.mult).then_inc(normed, 1)
                dve.wait_ge(normed, t.done(1, 2))
                nc.vector.bn_stats(stat[:, 1, :], xn[:, n_(t), :]).then_inc(stats_ready, 1)
                dve.wait_ge(stats_ready, t.done(3, 4))
                dve.sem_inc(passed, 1)
                nc.vector.bn_aggr(mv[:, 1, :], stat[:, 1, :]).then_inc(stats_ready, 1)

            def norm_branch(t):
                dve.wait_ge(rstd_ready, t.done(4, 4))
                if alive(t - 1):
                    dve.wait_ge(norm_turned, (t - 1).done())
                nc.vector.tensor_scalar(n0[:], xn[:, n_(t), :], mv[:, 1, 0:1], rstd[:, 1, 1:2],
                                        ALU.subtract, ALU.mult).then_inc(normed, 1)

            def block_rows(t, rows):
                def step(ins, done):
                    ins.then_inc(block_steps, 1)
                    dve.wait_ge(block_steps, t.done(done, 2 * BASE))

                if rows[0] == 0:
                    dve.wait_ge(blocks_in, t.done(16, 16))
                    if alive(t - 1):
                        dve.wait_ge(inverted_out, (t - 1).done(16, 16))
                    step(nc.vector.tensor_copy(blkT[:, 0], eye[:]), 1)
                for j in rows:
                    below, left = BASE - 1 - j, j + 1
                    step(nc.vector.tensor_tensor(
                        blkP[:, 0:below, 0:left],
                        blkM[:, j, left:BASE].unsqueeze(2).to_broadcast([NQ, below, left]),
                        blkT[:, 0, j, 0:left].unsqueeze(1).to_broadcast([NQ, below, left]), ALU.mult), 2 * j + 2)
                    step(nc.vector.tensor_tensor(blkT[:, 0, left:BASE, 0:left], blkT[:, 0, left:BASE, 0:left],
                                                 blkP[:, 0:below, 0:left], ALU.subtract), 2 * j + 3)
                if rows[-1] == BASE - 2:
                    nc.vector.tensor_copy(blkT[:, 1], blkT[:, 0].rearrange("q i j -> q j i")).then_inc(block_steps, 1)

            def start_z(t):
                dve.wait_ge(z_done, t.done())
                nc.vector.tensor_scalar(zm[:, 0:H + E], psL[:, 0:H + E], -80.0, None, ALU.max).then_inc(z_ready, 1)
                nc.vector.tensor_scalar(nz[:], psL[:, H + E:NZ], -1.0, 0.0, ALU.mult, ALU.max).then_inc(z_ready, 1)
                dve.wait_ge(z_ready, t.done(2, 3))
                nc.vector.scalar_tensor_tensor(zm[:, H + E:NZ], nz[:], 2.0, psL[:, H + E:NZ], ALU.mult, ALU.add).then_inc(z_ready, 1)

            def start_e1(t):
                dve.wait_ge(expz_ready, t.done())
                nc.vector.tensor_scalar(ez1[:], ez[:], 1.0, None, ALU.add).then_inc(sigmoid_ready, 1)
                dve.wait_ge(sigmoid_ready, t.done(1, 2))
                if alive((t - 2).group(1)):
                    dve.wait_ge(decay_ready, (t - 2).group(1).done())
                nc.vector.reciprocal(sg[:, t.const % 2, :], ez1[:, 0:H + E]).then_inc(sigmoid_ready, 1)

            def start_la(t):
                dve.wait_ge(logz_ready, t.done())
                if alive((t - 2).group(1)):
                    dve.wait_ge(rhsD_ready, (t - 2).group(1).done())
                nc.vector.tensor_tensor(la[:, t.const % 2, :], lnz[:], nz[:], ALU.add).then_inc(logalpha_ready, 1)

            def route(t):
                k = t.const % 2
                done = [0]

                def step(ins, alone=False):
                    ins.then_inc(routed, 1)
                    done[0] += 1
                    dve.wait_ge(routed, t.done(done[0], 32))
                    if alone:
                        dve.sem_inc(passed, 1)

                def choose(val, thr, k, n, dst):
                    step(nc.vector.tensor_scalar(gt[:, 0:n], val, thr, None, ALU.is_gt))
                    step(nc.vector.tensor_scalar(eq[:, 0:n], val, thr, None, ALU.is_equal))
                    step(nc.vector.tensor_reduce(cnt[:, 0:1], gt[:, 0:n], AX_X, ALU.add))
                    src, a, b = eqc, eqa, eqb
                    step(nc.vector.tensor_scalar(eqc[:, 16:16 + n], val, thr, None, ALU.is_equal))
                    shift = 1
                    while shift < n:
                        step(nc.vector.tensor_tensor(a[:, 16:16 + n], src[:, 16:16 + n],
                                                     src[:, 16 - shift:16 - shift + n], ALU.add))
                        src, a, b = a, b, a
                        shift *= 2
                    step(nc.vector.tensor_scalar(a[:, 16:16 + n], src[:, 16:16 + n], cnt[:, 0:1], k + 0.5,
                                                 ALU.add, ALU.is_lt))
                    step(nc.vector.tensor_tensor(a[:, 16:16 + n], a[:, 16:16 + n], eq[:, 0:n], ALU.mult))
                    step(nc.vector.tensor_tensor(dst, gt[:, 0:n], a[:, 16:16 + n], ALU.add))

                dve.wait_ge(sigmoid_ready, t.done(2, 2))
                step(nc.vector.tensor_tensor(sfc[:], sg[:, k, H:H + E], ecb_sb[:], ALU.add))
                groups = sfc[:].rearrange("p (g e) -> p g e", g=NG)
                step(nc.vector.tensor_reduce(gmx[:], groups, AX_X, ALU.max), alone=True)
                step(nc.vector.max(top[:], gmx[:]))
                choose(gmx[:], top[:, KG - 1:KG], KG, NG, gmask[:])
                step(nc.vector.tensor_tensor(masked[:].rearrange("p (g e) -> p g e", g=NG), groups,
                                             along(gmask[:], EG), ALU.mult), alone=True)
                step(nc.vector.max(top[:], masked[:]))
                choose(masked[:], top[:, TOPK - 1:TOPK], TOPK, E, chosen[:])
                step(nc.vector.tensor_tensor(wsel[:], chosen[:], sg[:, k, H:H + E], ALU.mult))
                step(nc.vector.tensor_reduce(wsum[:, 0:1], wsel[:], AX_X, ALU.add))
                step(nc.vector.tensor_scalar(wsum[:, 0:1], wsum[:, 0:1], 1e-20, None, ALU.add))
                step(nc.vector.reciprocal(wsum[:, 1:2], wsum[:, 0:1]))
                if alive((t - 2).group(1)):
                    dve.wait_ge(ehc_ready, (t - 2).group(1).done(2, 2))
                step(nc.vector.tensor_scalar(comb[:, k, :], wsel[:], wsum[:, 1:2], SCALE, ALU.mult, ALU.mult))
                assert done[0] == 32

            def sums(s):
                dve.wait_ge(squares_ready, s.done(2, 2))
                if alive(s - 1):
                    dve.wait_ge(norms_ready, (s - 1).done(5, 5))
                nc.vector.tensor_reduce(ssq[:], qk2[:].rearrange("p a (h d) -> p (a h) d", h=HALF), AX_X, ALU.add).then_inc(sums_ready, 1)

            def hats(s):
                dve.wait_ge(norms_ready, s.done(2, 5))
                if alive(s - 1):
                    dve.wait_ge(qg_turned, (s - 1).done())
                p = s.const % 2
                nc.vector.tensor_tensor(heads(hat[:, 0, :]), heads(qk[:, p, 1, :]), along(rn[:, 0, HALF:2 * HALF], P),
                                            ALU.mult).then_inc(hats_ready, 1)
                nc.vector.tensor_tensor(heads(hat[:, 1, :]), heads(qk[:, p, 0, :]), along(rn[:, 0, 0:HALF], P),
                                            ALU.mult).then_inc(hats_ready, 1)

            def copy_Tq(s):
                dve.wait_ge(q_turned, s.done())
                nc.vector.tensor_copy(kqT[:, s.const % 4, :, 1, :], heads(psA[0][:])).then_inc(qT_ready, 1)

            def products(s):
                r = s.const % 4
                dve.wait_ge(decay_ready, s.done())
                if alive(s - 4):
                    dve.wait_ge(OT_done, (s - 4).done())
                for part in range(2):
                    dve.wait_ge(products_done, s.done(part + 1, 2))
                    d = decay[:, part * 2 * P:(part + 1) * 2 * P].rearrange("p (h i) -> p h i", h=2)
                    nc.vector.tensor_tensor(
                        MA[:, r, 2 * part:2 * part + 2, :, :],
                        psA[part][:].rearrange("p (h a i) -> p h a i", h=2, a=2),
                        d.unsqueeze(2).to_broadcast([P, 2, 2, P]), ALU.mult).then_inc(MA_ready, 1)

            def inv_Q(s, l):
                dve.wait_ge(P_done, s.done(l + 1, NL))
                if l == 0:
                    if alive(s - 1):
                        dve.wait_ge(W_done, (s - 1).done(NL, NL))
                nc.vector.tensor_tensor(heads(Qm[:]), heads(psB[0][:]), across(level[:, l, :], HALF), ALU.mult).then_inc(Q_ready, 1)

            def rec_R(s):
                dve.wait_ge(KS_done, s.done())
                t = s.tile()
                for h in range(HALF):
                    c = slice(h * P, (h + 1) * P)
                    hh = (s.const % 2) * HALF + h
                    last = nc.vector.scalar_tensor_tensor(R[:, c], psC[0][:, c], dec[:, n_(t), hh:hh + 1],
                                                          v[:, s.const % 4, c], ALU.mult, ALU.subtract)
                last.then_inc(R_ready, 1)

            def rec_S(s):
                dve.wait_ge(dS_done, s.done())
                t = s.tile()
                for h in range(HALF):
                    c = slice(h * P, (h + 1) * P)
                    hh = (s.const % 2) * HALF + h
                    o = 2 * H + hh
                    last = nc.vector.scalar_tensor_tensor(S[:, t.const % B, hh, :], S[:, t.const % B, hh, :],
                                                          dec[:, n_(t), o:o + 1], psC[1][:, c], ALU.mult, ALU.add)
                last.then_inc(S_ready, 1)

            def expert_h(s, j):
                dve.wait_ge(eup_done, s.done(j + 1, 2))
                nc.vector.tensor_tensor(sgm[:, j, :], psM[:], sgm[:, j, :], ALU.mult).then_inc(eh_ready, 1)

            def expert_eT(s, j):
                dve.wait_ge(eh_turned, s.done(j + 1, 2))
                k = (2 * (s.const % 2) + j) * HALF
                nc.vector.tensor_copy(hT[:, k:k + HALF, :], heads(psM[:])).then_inc(ehT_ready, 1)

            def shared_h(s):
                dve.wait_ge(shgate_ready, s.tile().done())
                nc.vector.tensor_tensor(shh[:], psM[:, P:2 * P], shs[:], ALU.mult).then_inc(shh_ready, 1)

            def shared_eT(s):
                dve.wait_ge(shh_turned, s.tile().done())
                nc.vector.tensor_copy(hT[:, KT, :], psM[:, 0:P]).then_inc(shhT_ready, 1)

            def fin_norm(t):
                dve.wait_ge(x1_done, t.done())
                if alive(t - 1):
                    dve.wait_ge(x1b_ready, (t - 1).done())
                nc.vector.tensor_tensor(x1[:], psL[:, 256:384], xn[:, n_(t), :], ALU.add).then_inc(x1_ready, 1)
                dve.wait_ge(x1_ready, t.done())
                nc.vector.bn_stats(stat[:, 2, :], x1[:]).then_inc(x1stats_ready, 1)
                dve.wait_ge(x1stats_ready, t.done(1, 2))
                dve.sem_inc(passed, 1)
                nc.vector.bn_aggr(mv[:, 2, :], stat[:, 2, :]).then_inc(x1stats_ready, 1)

            def fin_h0(t):
                dve.wait_ge(x1rstd_ready, t.done(2, 2))
                nc.vector.tensor_scalar(h0[:], x1[:], mv[:, 2, 0:1], rstd[:, 2, 1:2], ALU.subtract, ALU.mult).then_inc(h0_ready, 1)

            def fin_hT(t):
                dve.wait_ge(h0_turned, t.done())
                nc.vector.tensor_scalar(hT2[:], psL[:, 384:512], ln2_sb[:, 0:1], ln2_sb[:, 1:2], ALU.mult, ALU.add).then_inc(hT_ready, 1)

            def fin_s(t):
                dve.wait_ge(w2_done, t.done())
                dve.wait_ge(x1b_ready, t.done())
                nc.vector.tensor_tensor(fs[:], psL[:, 256:384], x1b[:], ALU.add).then_inc(s_ready, 1)

            def slot(s):
                a = alive(s)
                bs, b = s - LAGB, alive(s - LAGB)
                cs, c = s - LAGC, alive(s - LAGC)
                even = s.const % 2 == 0
                f = even and alive(s - LAGF)
                ft = (s - LAGF).tile()
                nxt = (s + 1).tile()
                l = not even and alive(nxt, TILES)
                tile = (s - 2).tile()
                blocks = even and alive(tile, TILES)
                if l:
                    norm_stats(nxt)
                if c:
                    rec_R(cs)
                if a:
                    sums(s)
                if f:
                    fin_norm(ft)
                if l:
                    norm_input(nxt)
                if b:
                    inv_Q(bs, 0)
                if a:
                    hats(s)
                if l:
                    norm_branch(nxt)
                if f:
                    fin_h0(ft)
                if blocks:
                    block_rows(tile, range(0, 4))
                if b:
                    inv_Q(bs, 1)
                if a:
                    expert_h(s, 0)
                    copy_Tq(s)
                if blocks:
                    block_rows(tile, range(4, 8))
                if f:
                    fin_hT(ft)
                if c:
                    rec_S(cs)
                if l:
                    start_z(nxt)
                if b:
                    inv_Q(bs, 2)
                if blocks:
                    block_rows(tile, range(8, 12))
                if l:
                    start_e1(nxt)
                    start_la(nxt)
                if a:
                    expert_h(s, 1)
                if blocks:
                    block_rows(tile, range(12, BASE - 1))
                if a and even:
                    expert_eT(s, 0)
                if a and not even:
                    shared_h(s)
                if a:
                    products(s)
                    if even:
                        expert_eT(s, 1)
                    else:
                        expert_eT(s, 0)
                        expert_eT(s, 1)
                        shared_eT(s)
                if f:
                    fin_s(ft)
                if l:
                    route(nxt)

            slots(dve, begin, slot)

        @block.gpsimd
        def _(pool):
            def begin():
                pool.wait_ge(weights, n_weights)
                pool.wait_ge(constants_ready, 1)
                t = Stage(None, RING // 2, 0)
                start_rsqrt(t, 0)
                start_rsqrt(t, 1)

            def start_rsqrt(t, k):
                pool.wait_ge(stats_ready, t.done(2 * k + 2, 4))
                pool.sem_inc(passed, 1)
                nc.gpsimd.tensor_scalar(rstd[:, k, 0:1], mv[:, k, 1:2], EPS, None, ALU.add).then_inc(rstd_ready, 1)
                pool.wait_ge(rstd_ready, t.done(2 * k + 1, 4))
                nc.gpsimd.tensor_tensor(rstd[:, k, 1:2], rstd[:, k, 0:1], nhalf[:, 0:1], ALU.pow).then_inc(rstd_ready, 1)

            def fin_rsqrt(t):
                pool.wait_ge(x1stats_ready, t.done(2, 2))
                pool.sem_inc(passed, 1)
                nc.gpsimd.tensor_scalar(rstd[:, 2, 0:1], mv[:, 2, 1:2], EPS, None, ALU.add).then_inc(x1rstd_ready, 1)
                pool.wait_ge(x1rstd_ready, t.done(1, 2))
                nc.gpsimd.tensor_tensor(rstd[:, 2, 1:2], rstd[:, 2, 0:1], nhalf[:, 0:1], ALU.pow).then_inc(x1rstd_ready, 1)

            def squares(s):
                p = s.const % 2
                pool.wait_ge(k_ready, s.done())
                if alive(s - 1):
                    pool.wait_ge(sums_ready, (s - 1).done())
                for w in range(2):
                    nc.gpsimd.tensor_tensor(qk2[:, w, :], qk[:, p, w, :], qk[:, p, w, :], ALU.mult).then_inc(squares_ready, 1)

            def norms(s):
                t = s.tile()
                half = s.const % 2
                hs = slice(half * HALF, (half + 1) * HALF)
                pool.wait_ge(sums_ready, s.done())
                pool.wait_ge(decays_ready, t.done())
                if alive(s - 1):
                    pool.wait_ge(hats_ready, (s - 1).done(2, 2))
                pool.sem_inc(passed, 1)
                nc.gpsimd.tensor_scalar(rn[:, 1, :], ssq[:], L2EPS, None, ALU.add).then_inc(norms_ready, 1)
                pool.wait_ge(norms_ready, s.done(1, 5))
                nc.gpsimd.tensor_tensor(rn[:, 0, :], rn[:, 1, :], nhalf[:], ALU.pow).then_inc(norms_ready, 1)
                pool.wait_ge(norms_ready, s.done(2, 5))
                d = dec[:, n_(t), :]
                nc.gpsimd.tensor_tensor(rn[:, 2, 0:HALF], rn[:, 0, 0:HALF], d[:, hs], ALU.mult).then_inc(norms_ready, 1)
                nc.gpsimd.tensor_tensor(rn[:, 1, 0:HALF], rn[:, 0, HALF:2 * HALF],
                                            d[:, H + half * HALF:H + (half + 1) * HALF], ALU.mult).then_inc(norms_ready, 1)
                pool.wait_ge(norms_ready, s.done(4, 5))
                nc.gpsimd.tensor_tensor(rn[:, 2, HALF:2 * HALF], rn[:, 1, 0:HALF],
                                            sg[:, t.const % 2, hs], ALU.mult).then_inc(norms_ready, 1)
                pool.wait_ge(norms_ready, s.done(5, 5))

            def scale_q(s):
                if alive(s - 1):
                    pool.wait_ge(qg_turned, (s - 1).done())
                nc.gpsimd.tensor_tensor(heads(hat[:, 2, :]), heads(qk[:, s.const % 2, 0, :]),
                                        along(rn[:, 2, 0:HALF], P), ALU.mult).then_inc(qg_ready, 1)

            def scale_k(s):
                if alive(s - 4):
                    pool.wait_ge(dS_done, (s - 4).done())
                nc.gpsimd.tensor_tensor(heads(kdec[:, s.const % 4, :]), heads(qk[:, s.const % 2, 1, :]),
                                        along(rn[:, 2, HALF:2 * HALF], P), ALU.mult).then_inc(kdec_ready, 1)

            def rhs_D(s):
                t = s.tile()
                half = s.const % 2
                pool.wait_ge(logalpha_ready, t.done())
                if alive(s - 1):
                    pool.wait_ge(D_done, (s - 1).done())
                nc.gpsimd.tensor_tensor(heads(rhsD[:]), across(incl[:], HALF),
                                            along(la[:, t.const % 2, half * HALF:(half + 1) * HALF], P), ALU.mult).then_inc(rhsD_ready, 1)

            def beta_decay(s):
                t = s.tile()
                half = s.const % 2
                pool.wait_ge(expD_ready, s.done())
                if alive(s - 1):
                    pool.wait_ge(MA_ready, (s - 1).done(2, 2))
                nc.gpsimd.tensor_tensor(heads(decay[:]), heads(expD[:]),
                                            along(sg[:, t.const % 2, half * HALF:(half + 1) * HALF], P), ALU.mult).then_inc(decay_ready, 1)

            def diagonal(s):
                m = MA[:, s.const % 4, :, 0, :]
                pool.wait_ge(MA_ready, s.done(2, 2))
                pool.sem_inc(passed, 1)
                nc.gpsimd.affine_select(out=m, in_=m, compare_op=ALU.not_equal, fill=1.0, base=0,
                                            pattern=[[0, HALF], [-1, P]], channel_multiplier=1).then_inc(diagonal_set, 1)

            def expert_c(s, j):
                t = s.tile()
                k = 2 * (s.const % 2) + j
                ne = W4 // I
                pool.wait_ge(eh_ready, s.done(j + 1, 2))
                pool.wait_ge(routed, t.done(32, 32))
                nc.gpsimd.tensor_tensor(sgm[:, j, :].rearrange("p (e i) -> p e i", e=ne),
                                            sgm[:, j, :].rearrange("p (e i) -> p e i", e=ne),
                                            along(comb[:, t.const % 2, k * ne:(k + 1) * ne], I), ALU.mult).then_inc(ehc_ready, 1)

            def fin_bias(t):
                pool.wait_ge(x1_ready, t.done())
                if alive(t - 1):
                    pool.wait_ge(s_ready, (t - 1).done())
                nc.gpsimd.tensor_tensor(x1b[:], x1[:], b2_sb[:], ALU.add).then_inc(x1b_ready, 1)

            def fin_out(t):
                pool.wait_ge(s_ready, t.done())
                pool.wait_ge(branch_ready, t.done())
                nc.gpsimd.tensor_tensor(fy[:], fs[:], gsil[:, n_(t), :], ALU.mult).then_inc(y_ready, 1)
                pool.wait_ge(y_ready, t.done())
                if alive((t - 2).turn(2)):
                    pool.wait_ge(y_out[t.const % 2], (t - 2).turn(2).done(16, 16))
                pool.wait_ge(x_again[t.const % 2], t.turn(2).done(16, 16))
                nc.gpsimd.tensor_tensor(fo[:, t.const % 2, :], fy[:], xres[:, t.const % 2, :], ALU.add).then_inc(out_ready, 1)

            def slot(s):
                a = alive(s)
                bs, b = s - LAGB, alive(s - LAGB)
                cs, c = s - LAGC, alive(s - LAGC)
                even = s.const % 2 == 0
                f = even and alive(s - LAGF)
                ft = (s - LAGF).tile()
                nxt = (s + 1).tile()
                l = not even and alive(nxt, TILES)
                if l:
                    start_rsqrt(nxt, 0)
                if a:
                    squares(s)
                if f:
                    fin_rsqrt(ft)
                if l:
                    start_rsqrt(nxt, 1)
                if a:
                    norms(s)
                    rhs_D(s)
                    scale_q(s)
                    scale_k(s)
                if f:
                    fin_bias(ft)
                if a:
                    expert_c(s, 0)
                    beta_decay(s)
                    expert_c(s, 1)
                    diagonal(s)
                if f:
                    fin_out(ft)

            slots(pool, begin, slot)


def kernel(**inputs):
    import concourse.bacc as bacc
    from concourse.bass_utils import run_bass_kernel_spmd

    a = {k.replace("L0_attn_", "a_").replace("L0_ffn_", "f_"): np.asarray(v) for k, v in inputs.items()}
    D = a["a_x"].shape[-1]
    H = a["a_Wb"].shape[1]
    F = a["a_W1"].shape[1]
    E, two_i, _ = a["f_experts_gate_up"].shape
    I = two_i // 2
    put = np.ascontiguousarray
    i, j = np.arange(P)[:, None], np.arange(P)[None, :]
    level = np.zeros((P, len(LEVELS), P), np.float32)
    for n, s in enumerate(LEVELS):
        level[:, n, :] = (i == j) * 1.0 - ((i // (2 * s) == j // (2 * s)) & (i // s > j // s))
    arrays = dict(
        x=a["a_x"],
        wqkv=put(np.stack([a["a_Wq"], a["a_Wk"], a["a_Wv"]], 1)),
        wba=put(np.concatenate([a["a_Wb"], a["a_Wa"]], 1)),
        wo=put(a["a_Wo"].reshape(H, P, D).transpose(1, 0, 2)),
        ln1=put(np.stack([a["a_ln1_w"], a["a_ln1_b"]], 1)),
        ln2=put(np.stack([a["a_ln2_w"], a["a_ln2_b"]], 1)),
        w1=a["a_W1"],
        b1=put(a["a_b1"].reshape(F // P, P).T),
        w2=put(a["a_W2"].reshape(F // P, P, D).transpose(1, 0, 2)),
        b2=a["a_b2"],
        gate_t=put(a["f_gate_weight"].T),
        ecb=a["f_e_score_correction_bias"],
        gu=put(a["f_experts_gate_up"].reshape(E, 2, I, D).transpose(3, 1, 0, 2).reshape(D, 2, E * I)),
        down=put(a["f_experts_down"].transpose(0, 2, 1)),
        sh_gu=put(np.stack([a["f_shared_gate_w"].T, a["f_shared_up_w"].T], 1)),
        sh_down=put(a["f_shared_down_w"].T),
        c_ident=np.eye(P, dtype=np.float32),
        c_incl=(i <= j).astype(np.float32),
        c_after=(i > j).astype(np.float32),
        c_level=level,
        c_eye=put(np.broadcast_to(np.eye(BASE, dtype=np.float32), (P // BASE * H, BASE, BASE))),
    )
    nc = bacc.Bacc("TRN2", target_bir_lowering=False, num_devices=1)
    aps = {k: nc.dram_tensor(f"in_{k}", v.shape, mybir.dt.from_np(v.dtype), kind="ExternalInput").ap()
           for k, v in arrays.items()}
    out = nc.dram_tensor("out_y", a["a_x"].shape, F32, kind="ExternalOutput").ap()
    build(nc, **aps, out=out)
    r = run_bass_kernel_spmd(nc, [{f"in_{k}": v for k, v in arrays.items()}], core_ids=[0])
    return r.results[0]["out_y"]
```
